# Optimizing a Trainium2 kernel written in Bass

```python
import numpy as np
import jax
import jax.numpy as jnp

def _softmax(x, axis=-1):
    return jax.nn.softmax(x, axis=axis)

def _gelu(x):
    return jax.nn.gelu(x, approximate=True)

def _silu(x):
    return jax.nn.silu(x)

def _sigmoid(x):
    return jax.nn.sigmoid(x)

def _layernorm(x, axis=-1, eps=1e-05):
    m = jnp.mean(x, axis=axis, keepdims=True)
    v = jnp.var(x, axis=axis, keepdims=True)
    return (x - m) / jnp.sqrt(v + eps)

def _scatter_add(tgt, idx, src, axis=0):
    return tgt.at[idx].add(src)

def _segment_sum(src, seg, n):
    return jax.ops.segment_sum(src, seg, n)
kernel_name = 'mk_perceiver_d1_seqx_r4_82156e'

def setup_inputs(seed: int=0):
    np.random.seed(seed)
    _w = jnp.asarray

    def _rec_inputs():
        import jax
        import jax.numpy as jnp
        _rk = jax.random.key(seed)
        x = 0.0002417 + 0.9998 * jax.random.normal(jax.random.fold_in(_rk, 1), (64, 32, 256), jnp.float32)
        _lenS = 32 - jax.random.randint(jax.random.fold_in(_rk, 7), (64,), 0, max(1, 32 // 4) + 1, jnp.int32)
        _lenS2 = 257 - jax.random.randint(jax.random.fold_in(_rk, 8), (64,), 0, max(1, 257 // 4) + 1, jnp.int32)
        _ctx_1024P = jax.random.normal(jax.random.fold_in(_rk, 11), (64, 16, 256), jnp.float32)
        _ctx_1024c = jax.random.dirichlet(jax.random.fold_in(_rk, 511), 0.3 * jnp.ones((16,), jnp.float32), (64, 257))
        _ctx_1024t = jnp.einsum('bsk,bkd->bsd', _ctx_1024c, _ctx_1024P)
        _ctx_1024t = _ctx_1024t * jax.lax.rsqrt(jnp.mean(jnp.square(_ctx_1024t)) + 1e-12) * 0.953939
        ctx_1024 = 7.22013e-05 + 1.00017 * (_ctx_1024t + 0.3 * jax.random.normal(jax.random.fold_in(_rk, 611), (64, 257, 256), jnp.float32))
        return (x, ctx_1024)
    x, ctx_1024 = _rec_inputs()

    def _L0_xattn_setup():
        import jax, jax.numpy as jnp
        import numpy as np
        D_MODEL = 256
        B, S = (4, 512)
        key = jax.random.key(seed)
        ks = jax.random.split(key, 10)
        s = 1.0 / np.sqrt(D_MODEL)
        return {'k': jax.random.normal(ks[0], (B, S, D_MODEL), jnp.float32), 'v': jax.random.normal(ks[1], (B, S, D_MODEL), jnp.float32), 'q': jax.random.normal(ks[2], (B, S, D_MODEL), jnp.float32), 'Wk': jax.random.normal(ks[3], (D_MODEL, D_MODEL), jnp.float32) * s, 'Wv': jax.random.normal(ks[4], (D_MODEL, D_MODEL), jnp.float32) * s, 'bv': jnp.zeros((D_MODEL,), jnp.float32), 'Wq': jax.random.normal(ks[5], (D_MODEL, D_MODEL), jnp.float32) * s, 'bq': jnp.zeros((D_MODEL,), jnp.float32), 'Wo': jax.random.normal(ks[6], (D_MODEL, D_MODEL), jnp.float32) * s, 'bo': jnp.zeros((D_MODEL,), jnp.float32)}
    _L0_xattn_all = _L0_xattn_setup()
    _L0_xattn_in = {k: v for k, v in _L0_xattn_all.items() if k in ('Wk', 'Wv', 'bv', 'Wq', 'bq', 'Wo', 'bo')}
    del _L0_xattn_all

    def _L0_attn_setup():
        import jax, jax.numpy as jnp
        import numpy as np
        B, T, DIM = (2, 256, 256)
        H, D = (16, 64)
        key = jax.random.key(seed)
        k1, k2, k3, k4 = jax.random.split(key, 4)
        s = DIM ** (-0.5)
        return {'x': jax.random.normal(k1, (B, T, DIM), jnp.float32), 'w_qkv': jax.random.normal(k2, (DIM, 3 * H * D), jnp.float32) * s, 'w_gate': jax.random.normal(k3, (DIM, H * D), jnp.float32) * s, 'w_out': jax.random.normal(k4, (H * D, DIM), jnp.float32) * s}
    _L0_attn_all = _L0_attn_setup()
    _L0_attn_in = {k: v for k, v in _L0_attn_all.items() if k in ('w_qkv', 'w_gate', 'w_out')}
    del _L0_attn_all

    def _L0_ffn_setup():
        import jax, jax.numpy as jnp
        import numpy as np
        NUM_EXPERTS = 8
        TOP_K = 2
        DIM = 256
        HIDDEN = 1024
        B, S = (2, 256)
        key = jax.random.key(seed)
        k_x, k_g, k_1, k_2, k_3 = jax.random.split(key, 5)
        s_d = 1.0 / np.sqrt(DIM)
        s_h = 1.0 / np.sqrt(HIDDEN)
        return {'x': jax.random.normal(k_x, (B, S, DIM), dtype=jnp.float32), 'gate_w': jax.random.normal(k_g, (NUM_EXPERTS, DIM), dtype=jnp.float32) * s_d, 'w1': jax.random.normal(k_1, (NUM_EXPERTS, HIDDEN, DIM), dtype=jnp.float32) * s_d, 'w2': jax.random.normal(k_2, (NUM_EXPERTS, DIM, HIDDEN), dtype=jnp.float32) * s_h, 'w3': jax.random.normal(k_3, (NUM_EXPERTS, HIDDEN, DIM), dtype=jnp.float32) * s_d}
    _L0_ffn_all = _L0_ffn_setup()
    _L0_ffn_in = {k: v for k, v in _L0_ffn_all.items() if k in ('gate_w', 'w1', 'w2', 'w3')}
    del _L0_ffn_all
    return {'x': x, 'ctx_1024': ctx_1024, 'L0_xattn_Wk': _L0_xattn_in['Wk'], 'L0_xattn_Wv': _L0_xattn_in['Wv'], 'L0_xattn_bv': _L0_xattn_in['bv'], 'L0_xattn_Wq': _L0_xattn_in['Wq'], 'L0_xattn_bq': _L0_xattn_in['bq'], 'L0_xattn_Wo': _L0_xattn_in['Wo'], 'L0_xattn_bo': _L0_xattn_in['bo'], 'L0_attn_w_qkv': _L0_attn_in['w_qkv'], 'L0_attn_w_gate': _L0_attn_in['w_gate'], 'L0_attn_w_out': _L0_attn_in['w_out'], 'L0_ffn_gate_w': _L0_ffn_in['gate_w'], 'L0_ffn_w1': _L0_ffn_in['w1'], 'L0_ffn_w2': _L0_ffn_in['w2'], 'L0_ffn_w3': _L0_ffn_in['w3']}

def reference(x, ctx_1024, L0_xattn_Wk, L0_xattn_Wv, L0_xattn_bv, L0_xattn_Wq, L0_xattn_bq, L0_xattn_Wo, L0_xattn_bo, L0_attn_w_qkv, L0_attn_w_gate, L0_attn_w_out, L0_ffn_gate_w, L0_ffn_w1, L0_ffn_w2, L0_ffn_w3):
    import jax
    import jax.numpy as jnp

    def _L0_xattn_ref(k, v, q, Wk, Wv, bv, Wq, bq, Wo, bo):
        import jax, jax.numpy as jnp
        import numpy as np
        D_MODEL = 256
        B, S = (4, 512)
        kp = jnp.einsum('bsd,ed->bse', k, Wk)
        vp = jnp.einsum('bsd,ed->bse', v, Wv) + bv
        qp = jnp.einsum('bsd,ed->bse', q, Wq) + bq
        scale = 1.0 / jnp.sqrt(jnp.float32(kp.shape[-1]))
        scores = jnp.einsum('bqd,bkd->bqk', qp, kp) * scale
        probs = jax.nn.softmax(scores, axis=-1)
        ctx = jnp.einsum('bqk,bkd->bqd', probs, vp)
        return jnp.einsum('bqd,ed->bqe', ctx, Wo) + bo

    def _L0_attn_ref(x, w_qkv, w_gate, w_out):
        import jax, jax.numpy as jnp
        import numpy as np
        B, T, DIM = (2, 256, 256)
        H, D = (16, 64)
        b, t, c = x.shape
        qkv = (x @ w_qkv).reshape(b, t, 3, H, D)
        q, k, v = (qkv[:, :, 0], qkv[:, :, 1], qkv[:, :, 2])
        gate = jax.nn.sigmoid((x @ w_gate).reshape(b, t, H, D))
        q = jax.nn.elu(q) + 1.0
        k = jax.nn.elu(k) + 1.0
        k_cum = jnp.cumsum(k, axis=1)
        kv = jnp.cumsum(k[..., None, :] * v[..., :, None], axis=1)
        numerator = jnp.einsum('bthj,bthij->bthi', q, kv)
        denominator = jnp.einsum('bthj,bthj->bth', q, k_cum)
        out = numerator / (denominator[..., None] + 1e-06)
        out = out * gate
        return out.reshape(b, t, H * D) @ w_out

    def _L0_ffn_ref(x, gate_w, w1, w2, w3):
        import jax, jax.numpy as jnp
        import numpy as np
        NUM_EXPERTS = 8
        TOP_K = 2
        DIM = 256
        HIDDEN = 1024
        B, S = (2, 256)
        orig_shape = x.shape
        xt = x.reshape(-1, orig_shape[-1])
        scores = xt @ gate_w.T
        top_vals, top_idx = jax.lax.top_k(scores, TOP_K)
        top_w = jax.nn.softmax(top_vals, axis=-1)
        combine = jnp.einsum('tke,tk->te', jax.nn.one_hot(top_idx, NUM_EXPERTS, dtype=xt.dtype), top_w)
        h = jax.nn.silu(jnp.einsum('td,ehd->eth', xt, w1)) * jnp.einsum('td,ehd->eth', xt, w3)
        ye = jnp.einsum('eth,edh->etd', h, w2)
        y = jnp.einsum('te,etd->td', combine, ye)
        return y.reshape(orig_shape)
    x = x + _L0_xattn_ref(ctx_1024, ctx_1024, _layernorm(x, axis=-1), L0_xattn_Wk, L0_xattn_Wv, L0_xattn_bv, L0_xattn_Wq, L0_xattn_bq, L0_xattn_Wo, L0_xattn_bo)
    x = x + _L0_attn_ref(_layernorm(x, axis=-1), L0_attn_w_qkv, L0_attn_w_gate, L0_attn_w_out)
    x = x + _L0_ffn_ref(_layernorm(x, axis=-1), L0_ffn_gate_w, L0_ffn_w1, L0_ffn_w2, L0_ffn_w3)
    return x

_drawn_inputs = setup_inputs


def setup_inputs(seed=0):
    import zlib

    import numpy as np

    out = dict(_drawn_inputs(seed))
    spreads = {'L0_xattn_bv': (0.0, 0.1), 'L0_xattn_bq': (0.0, 0.1), 'L0_xattn_bo': (0.0, 0.1)}
    factors = {}
    for name, (base, spread) in spreads.items():
        noise = np.random.default_rng([zlib.crc32(name.encode()), seed]).standard_normal(out[name].shape)
        drawn = base * np.exp(spread * noise) if base else spread * noise
        out[name] = jnp.asarray(drawn.astype(out[name].dtype))
    for name, factor in factors.items():
        out[name] = (out[name] * factor).astype(out[name].dtype)
    return out
```

```python
from contextlib import ExitStack

import numpy as np

import concourse.bass as bass
from concourse import mybir

F32 = mybir.dt.float32
F32R = mybir.dt.float32r
I32 = mybir.dt.int32
U32 = mybir.dt.uint32
ALU = mybir.AluOpType
ACT = mybir.ActivationFunctionType
AX = mybir.AxisListType

P = 128
B, T, D = 64, 32, 256
S = 257
DC = D // P
BT = P // T
NT = B // BT
KC = S // P
H, HD = 16, 64
HF = H * HD
FC = HF // P
E, HID = 8, 1024
HC = HID // P
TOP = 2
SLOT_TILES = (TOP * NT * P + E * (P - 1)) // P
SLOTS = SLOT_TILES * P
MAXT = NT
LN_EPS = 1e-5
DEN_EPS = 1e-6
V1 = HD + 1

C_ID = 0
C_MASK = C_ID + P
C_LOW = C_MASK + P
C_ONES = C_LOW + P
C_BATCH = C_ONES + P
C_IOTA = C_BATCH + BT
C_STEP = C_IOTA + E
C_TILE = C_STEP + MAXT
C_END = C_TILE + SLOT_TILES


def constants():
    c = np.zeros((P, C_END), np.float32)
    p = np.arange(P)
    c[:, C_ID:C_ID + P] = p[:, None] == p[None, :]
    c[:, C_MASK:C_MASK + P] = (p[:, None] // T == p[None, :] // T) & (p[:, None] <= p[None, :])
    c[:, C_LOW:C_LOW + P] = p[:, None] < p[None, :]
    c[:, C_ONES:C_ONES + P] = 1.0
    c[:, C_BATCH:C_BATCH + BT] = p[:, None] // T == np.arange(BT)[None, :]
    c[:, C_IOTA:C_IOTA + E] = np.arange(E)
    c[:, C_STEP:C_STEP + MAXT] = P * np.arange(MAXT)
    c[:, C_TILE:C_TILE + SLOT_TILES] = np.arange(SLOT_TILES)
    return c


def wait(eng, sem, value):
    if isinstance(value, int) and value <= 0:
        return
    eng.wait_ge(sem, value)


def skewed(eng, step, first, lo, hi, last):
    for t in range(first, lo):
        step(t, t % 2)
    with eng.Fori(0, (hi - lo) // 2) as i:
        for u in range(2):
            step(lo + 2 * i + u, (lo + u) % 2)
    for t in range(hi, last):
        step(t, t % 2)


def valid(t, n):
    return not isinstance(t, int) or 0 <= t < n


def program(nc, a, out):
    with ExitStack() as ctx:
        build(nc, ctx, a, out)


def build(nc, ctx, a, out):
    BASE = 16512
    TOP_ADDR = 229344
    EXP_BYTES = 2 * DC * HID * 4
    W13_AT = TOP_ADDR - E * EXP_BYTES
    EARLY = 2
    LATE_AT = W13_AT + EARLY * EXP_BYTES
    slab = ctx.enter_context(nc.sbuf_tensor("slab", [P, (TOP_ADDR - BASE) // 4], F32))
    at = {"low": BASE, "late": LATE_AT}

    def place(name, shape, dtype=F32, where="low"):
        n = 4
        for d in shape[1:]:
            n *= d
        t = nc.alloc_sbuf_tensor_at(name, shape, dtype, offset=at[where])
        at[where] += (n + 31) // 32 * 32
        return t

    con = place("con", [P, C_END])
    x_all = place("x_all", [P, NT, D])
    bn6 = [place(f"bn6_{i}", [P, NT, 6]) for i in range(3)]
    mean = [place(f"mean{i}", [P, NT]) for i in range(3)]
    rstd = [place(f"rstd{i}", [P, NT]) for i in range(3)]
    half = place("half", [P, NT])
    sq = place("sq", [P, NT])
    eps = place("eps", [P, 1])
    gw = place("gw", [P, DC, E])
    w_out = place("w_out", [P, FC, D])
    top_w = place("top_w", [P, TOP, NT])
    pos = place("pos", [P, TOP, NT], I32)
    tile_e = place("tile_e", [P, SLOT_TILES], I32)
    shared = at["low"]

    w13 = nc.alloc_sbuf_tensor_at("w13", [P, E, 2, DC, HID], F32, offset=W13_AT)
    ident = con[:, C_ID:C_ID + P]
    ones = con[:, C_ONES:C_ONES + P]

    wa_hi = nc.alloc_sbuf_tensor_at("wa_hi", [P, DC, 4 * HF], F32R, offset=TOP_ADDR - 2 * DC * 4 * HF * 4)
    wa_lo = nc.alloc_sbuf_tensor_at("wa_lo", [P, DC, 4 * HF], F32R, offset=TOP_ADDR - DC * 4 * HF * 4)
    SW = 512
    NPIECE = DC * 4 * HF // SW
    assert NPIECE == NT
    wq = place("wq", [P, DC, D], where="late")
    wk = place("wk", [P, DC, D], where="late")
    wv = place("wv", [P, DC, D], where="late")
    wo = place("wo", [P, DC, D], where="late")
    stage = place("stage", [P, 2, SW], where="late")
    ctx_n = place("ctx_n", [P, 2, BT, KC, D], where="late")
    ctx_t = place("ctx_t", [P, 2, BT, DC, S])
    ctx_l = place("ctx_l", [BT, 2, D])
    bqc = place("bqc", [P, DC])
    bvc = place("bvc", [P, DC])
    bor = place("bor", [1, D])
    bvb = place("bvb", [P, DC, P])
    m_qk = place("m_qk", [P, DC, D])
    c_qk = place("c_qk", [P, DC])
    w_vo = place("w_vo", [P, DC, D])
    bias = place("bias", [P, D])
    xn = place("xn", [P, 2, D])
    xnT = place("xnT", [P, 2, DC, P])
    qkT = place("qkT", [P, 2, DC, P])
    mx = place("mx", [P, 2, 1])
    nmx = place("nmx", [P, 2, 1])
    rs = place("rs", [P, 2, 1])
    rrs = place("rrs", [P, 2, 1])
    prob = place("prob", [P, 2, S + 3])
    p_last = place("p_last", [P, 2, BT])
    pT = place("pT", [P, 2, KC, P])
    pTl = place("pTl", [BT, 2, P])
    cn = place("cn", [P, D])
    cT = place("cT", [P, DC, P])
    ZC = 3 * D
    zero = place("zero", [P, ZC])
    assert at["low"] <= W13_AT and at["late"] <= TOP_ADDR - 2 * DC * 4 * HF * 4, (at, W13_AT)

    at["low"], at["late"] = shared, LATE_AT
    q_pad = place("q_pad", [P, FC, 2, 2, P], where="late")
    att = place("att", [P, 2, H, P], where="late")
    assert at["late"] <= TOP_ADDR - 2 * DC * 4 * HF * 4
    kT = place("kT", [P, FC, 2 * P])
    xT_hi = place("xT_hi", [P, DC, 2 * P], F32R)
    xT_lo = place("xT_lo", [P, DC, 2 * P], F32R)
    VW = H * V1 + P - V1
    v_one = place("v_one", [P, 2, VW])
    eg = place("eg", [P, 2, HF])
    o_sb = place("o_sb", [P, 2, HF])
    oT = place("oT", [P, FC, P])
    ex = place("ex", [P, 2, 512])
    xn2 = place("xn2", [P, 2, D])
    dn = place("dn", [P, 4, 1])
    dg = place("dg", [P, 4, HD])
    rdg = place("rdg", [P, 4, HD])
    assert at["low"] <= W13_AT, (at, W13_AT)

    at["low"] = shared
    xn3 = place("xn3", [P, 2, D])
    xn3_all = place("xn3_all", [P, NT, D])
    xT3 = place("xT3", [P, 2, DC, P])
    sc = place("sc", [P, NT, E])
    m8 = place("m8", [P, NT, 8])
    i8 = place("i8", [P, NT, 8], U32)
    i8f = place("i8f", [P, NT, 8])
    first = place("first", [P, NT, E])
    second = place("second", [P, NT, E])
    both = place("both", [P, NT, E])
    scan = [place(f"scan{i}", [P, NT + 8, E]) for i in range(2)]
    cmp = place("cmp", [P, E, MAXT])
    tiles = [place(f"tiles{i}", [P, 4 + E]) for i in range(2)]
    slot = place("slot", [P, NT, E])
    prod = place("prod", [P, NT, E])
    posf = place("posf", [P, TOP, NT])
    cmp2 = place("cmp2", [P, SLOT_TILES, E])
    tef = place("tef", [P, SLOT_TILES])
    dv = place("dv", [P, NT])
    e1 = place("e1", [P, NT])
    xs_sb = place("xs_sb", [P, D])
    xT4 = place("xT4", [P, DC, P])
    sl = place("sl", [P, HID])
    h_sb = place("h_sb", [P, HID])
    hT = place("hT", [P, HC, P])
    w2_sb = place("w2_sb", [P, HC, D])
    y_sb = place("y_sb", [P, D])
    assert at["low"] <= W13_AT, (at, W13_AT)
    at["late"] = LATE_AT
    gat = place("gat", [P, TOP, NT, D], where="late")

    ps = ctx.enter_context(nc.psum_tensor("ps", [P, 8, 512], F32))

    xs = nc.dram_tensor("xs", (SLOTS, D), F32, kind="Internal").ap()
    ys = nc.dram_tensor("ys", (SLOTS, D), F32, kind="Internal").ap()

    def sem(name):
        return ctx.enter_context(nc.semaphore(name))

    l_con, l_wx, l_x, l_wo, l_z = (sem(n) for n in ("l_con", "l_wx", "l_x", "l_wo", "l_z"))
    l_stage = [sem("l_stage0"), sem("l_stage1")]
    l_ctx = [sem("l_ctx0"), sem("l_ctx1")]
    l_w13 = sem("l_w13")
    s_st, s_var, s_part, s_sqrt, s_rstd, s_bvb, s_mm, s_ev, s_zero, s_split_hi, s_split_lo = (
        sem(n) for n in ("s_st", "s_var", "s_part", "s_sqrt", "s_rstd", "s_bvb", "s_mm", "s_ev", "s_zero", "s_split_hi", "s_split_lo"))
    (x_ln, x_tr, x_xnT, x_qk, x_qkT, x_sc, x_max, x_nmax, x_exp, x_plast, x_pt, x_pT, x_pv, x_norm, x_ct, x_cT,
     x_out, x_bias, x_x1, x_bn) = (sem("x_" + n) for n in (
         "ln", "tr", "xnT", "qk", "qkT", "sc", "max", "nmax", "exp", "plast", "pt", "pT", "pv", "norm", "ct", "cT",
         "out", "bias", "x1", "bn"))
    (a_init, a_ln, a_tr, a_hi, a_lo, a_qk, a_e, a_emin, a_qku, a_vg, a_vgu, a_sc, a_scu, a_av, a_dn, a_dg, a_rdg,
     a_avu, a_ot, a_oT, a_y, a_x2, a_bn) = (sem("a_" + n) for n in (
         "init", "ln", "tr", "hi", "lo", "qk", "e", "emin", "qk_used", "vg", "vg_used", "sc", "sc_used", "av", "dn",
         "dg", "rdg", "av_used", "ot", "oT", "y", "x2", "bn"))
    g_ln, g_keep, g_tr, g_xT, g_mm, g_sc, g_max, g_idx, r_step, r_d, r_e1, r_sum, r_pos, r_map, r_scat = (
        sem(n) for n in ("g_ln", "g_keep", "g_tr", "g_xT", "g_mm", "g_sc", "g_max", "g_idx", "r_step", "r_d", "r_e1",
                         "r_sum", "r_pos", "r_map", "r_scat"))
    f_xs, f_w2, f_xtr, f_xT, f_up, f_silu, f_h, f_t, f_hT, f_y, f_yev, f_st = (
        sem("f_" + n) for n in ("xs", "w2", "xtr", "xT", "up", "silu", "h", "t", "hT", "y", "yev", "st"))
    o_gat = [sem(f"o_gat{t}") for t in range(NT)]
    o_mix, o_sum, o_st = (sem("o_" + n) for n in ("mix", "sum", "st"))

    block = ctx.enter_context(nc.Block())
    X_LO, X_HI = 4, 12

    @block.sync
    def _(sp):
        sp.dma_start(con[:, :], a["con"]).then_inc(l_con, 16)
        sp.dma_start(x_all[:, :, :], a["x"]).then_inc(l_x, 16)
        for buf, name in ((wq, "Wq"), (wk, "Wk"), (wv, "Wv"), (wo, "WoT")):
            sp.dma_start(buf[:, :, :], a[name].rearrange("(c p) n -> p c n", p=P)).then_inc(l_wx, 16)
        for buf, name in ((bqc, "bq"), (bvc, "bv"), (bor, "bo")):
            sp.dma_start(buf[:, :], a[name]).then_inc(l_wx, 16)

        def load(t, p):
            if not valid(t, NT):
                return
            wait(sp, x_pv, t - 1)
            sp.dma_start(ctx_t[:, p, :, :, :].rearrange("p b c s -> p (b c s)"), a["ctxT"][t, :, :]).then_inc(l_ctx[p], 16)
            sp.dma_start(ctx_n[:, p, :, :, :].rearrange("p b c d -> p (b c d)"), a["ctxN"][t, :, :]).then_inc(l_ctx[p], 16)
            sp.dma_start(ctx_l[:, p, :], a["ctxL"][t, :, :]).then_inc(l_ctx[p], 16)
            wait(sp, s_split_lo, t - 1)
            sp.dma_start(stage[:, p, :], a["w_a"][:, bass.ds(t * SW, SW)]).then_inc(l_stage[p], 16)

        for t in range(2):
            load(t, t)
        sp.dma_start(w_out[:, :, :], a["w_out"].rearrange("(c p) n -> p c n", p=P)).then_inc(l_wo, 16)
        sp.dma_start(gw[:, :, :], a["gate"].rearrange("(c p) n -> p c n", p=P)).then_inc(l_wo, 16)
        for t in range(2, X_LO):
            load(t, t % 2)
        with sp.Fori(0, (X_HI - X_LO) // 2) as i:
            for u in range(2):
                load(X_LO + 2 * i + u, u)
        for t in range(X_HI, NT):
            load(t, t % 2)
        sp.dma_start(w13[:, 0:EARLY, :, :, :].rearrange("p e w c h -> p e (w c h)"),
                     a["w13"][0:EARLY, :, :].rearrange("e p n -> p e n")).then_inc(l_w13, 16)
        sp.wait_ge(a_x2, NT)
        for e in range(EARLY, E):
            sp.dma_start(w13[:, e, :, :, :].rearrange("p w c h -> p (w c h)"), a["w13"][e, :, :]).then_inc(l_w13, 16)

        def load_rows(t):
            if valid(t, SLOT_TILES):
                wait(sp, f_xtr, t)
                sp.dma_start(xs_sb[:, :], xs[bass.ds(t * P, P), :]).then_inc(f_xs, 16)

        def load_w2(t):
            if valid(t, SLOT_TILES):
                e = sp.value_load(tile_e[0:1, bass.ds(t, 1)], min_val=0, max_val=E - 1)
                wait(sp, f_y, t)
                sp.dma_start(w2_sb[:, :, :].rearrange("p c d -> p (c d)"), a["w2"][bass.ds(e, 1), :, :].rearrange("e p n -> (e p) n")).then_inc(f_w2, 16)

        def store_y(t):
            if valid(t, SLOT_TILES):
                wait(sp, f_yev, t + 1)
                sp.dma_start(ys[bass.ds(t * P, P), :], y_sb[:, :]).then_inc(f_st, 16)

        def step(t):
            load_rows(t + 2)
            load_w2(t)
            store_y(t - 1)

        sp.wait_ge(r_scat, 16 * TOP * NT)
        sp.wait_ge(r_map, 1)
        load_rows(0)
        load_rows(1)
        step(0)
        with sp.Fori(1, SLOT_TILES - 2) as t:
            step(t)
        for t in range(SLOT_TILES - 2, SLOT_TILES + 1):
            step(t)
        for q in range(4):
            n = NT // 4
            sp.wait_ge(o_sum, n * (q + 1))
            sp.dma_start(out[:, q * n:(q + 1) * n, :], x_all[:, q * n:(q + 1) * n, :]).then_inc(o_st, 16)
        sp.wait_ge(o_st, 64)

    @block.gpsimd
    def _(pool):
        pool.memset(zero[:, :], 0.0).then_inc(s_zero, 1)
        pool.wait_ge(s_zero, 1)
        xs_p = xs.rearrange("(p n) d -> p (n d)", p=P)
        for j in range(SLOT_TILES * D // ZC):
            pool.dma_start(xs_p[:, j * ZC:(j + 1) * ZC], zero[:, :]).then_inc(l_z, 16)
        pool.wait_ge(s_ev, 6)
        hi_all = wa_hi[:, :, :].rearrange("p c n -> p (c n)")
        lo_all = wa_lo[:, :, :].rearrange("p c n -> p (c n)")
        with pool.Fori(0, NT // 2) as i:
            for p in range(2):
                t = 2 * i + p
                pool.wait_ge(x_ln, t + 1)
                row = x_all[:, bass.ds(t, 1), :].rearrange("p a d -> p (a d)")
                pool.tensor_tensor(row, row, bias[:, :], ALU.add).then_inc(x_bias, 1)
                pool.wait_ge(l_stage[p], 16 * i + 16)
                pool.tensor_copy(hi_all[:, bass.ds(t * SW, SW)], stage[:, p, :]).then_inc(s_split_hi, 1)
                pool.wait_ge(s_split_hi, t + 1)
                pool.tensor_tensor(lo_all[:, bass.ds(t * SW, SW)], stage[:, p, :],
                                   hi_all[:, bass.ds(t * SW, SW)].bitcast(F32), ALU.subtract).then_inc(s_split_lo, 1)
        pool.wait_ge(l_z, 16 * (SLOT_TILES * D // ZC))
        pool.wait_ge(r_pos, 1)
        pool.wait_ge(g_keep, NT)
        for t in range(NT):
            for k in range(TOP):
                pool.indirect_dma_start(xs, bass.IndirectOffsetOnAxis(pos[:, k, t:t + 1], 0), xn3_all[:, t, :], None).then_inc(r_scat, 16)
        pool.wait_ge(f_st, 16 * SLOT_TILES)
        for t in range(NT):
            for k in range(TOP):
                pool.indirect_dma_start(gat[:, k, t, :], None, ys, bass.IndirectOffsetOnAxis(pos[:, k, t:t + 1], 0)).then_inc(o_gat[t], 16)

    @block.tensor
    def _(pe):
        def mm3(dst, l_hi, l_lo, r_hi, r_lo, first, last):
            pe.matmul(dst, l_hi, r_hi, start=first, stop=False)
            pe.matmul(dst, l_hi, r_lo, start=False, stop=False)
            return pe.matmul(dst, l_lo, r_hi, start=False, stop=last)

        pe.wait_ge(l_wx, 16 * 7)
        pe.wait_ge(l_con, 16)
        for dc in range(DC):
            for ec in range(DC):
                m = pe.matmul(ps[:, 0, dc * D:(dc + 1) * D], wq[:, ec, dc * P:(dc + 1) * P], wk[:, ec, :],
                              start=ec == 0, stop=ec == DC - 1)
        m.then_inc(s_mm, 1)
        for dc in range(DC):
            for ec in range(DC):
                m = pe.matmul(ps[:, 1, dc:dc + 1], wk[:, ec, dc * P:(dc + 1) * P], bqc[:, ec:ec + 1],
                              start=ec == 0, stop=ec == DC - 1)
        m.then_inc(s_mm, 1)
        for dc in range(DC):
            for ec in range(DC):
                m = pe.matmul(ps[:, 2, dc * D:(dc + 1) * D], wv[:, ec, dc * P:(dc + 1) * P], wo[:, ec, :],
                              start=ec == 0, stop=ec == DC - 1)
        m.then_inc(s_mm, 1)
        pe.wait_ge(s_bvb, DC)
        for ec in range(DC):
            pe.matmul(ps[:, 3, 0:D], bvb[:, ec, :], wo[:, ec, :], start=ec == 0, stop=False)
        pe.matmul(ps[:, 3, 0:D], ones[0:1, :], bor[0:1, :], start=False, stop=True).then_inc(s_mm, 1)
        pe.wait_ge(s_ev, 6)

        def tr(t, p):
            if not valid(t, NT):
                return
            wait(pe, x_ln, t + 1)
            wait(pe, x_xnT, t)
            for dc in range(DC):
                m = pe.transpose(ps[:, 2, dc * P:(dc + 1) * P], xn[:, p, dc * P:(dc + 1) * P], ident)
            m.then_inc(x_tr, 1)

        def qk(t, p):
            if not valid(t, NT):
                return
            wait(pe, x_xnT, t + 1)
            wait(pe, x_qkT, t)
            for oc in range(DC):
                for dc in range(DC):
                    m = pe.matmul(ps[:, 3, oc * P:(oc + 1) * P], m_qk[:, dc, oc * P:(oc + 1) * P], xnT[:, p, dc, :],
                                  start=dc == 0, stop=dc == DC - 1)
            m.then_inc(x_qk, 1)

        def scores(t, p):
            if not valid(t, NT):
                return
            pe.wait_ge(l_ctx[p], 48 * (t // 2 + 1) if isinstance(t, int) else 24 * (t - p) + 48)
            wait(pe, x_qkT, t + 1)
            wait(pe, x_exp, t - 1)
            for dc in range(DC):
                for b in range(BT):
                    m = pe.matmul(ps[b * T:(b + 1) * T, p, 0:S], qkT[:, p, dc, b * T:(b + 1) * T], ctx_t[:, p, b, dc, :],
                                  start=dc == 0, stop=dc == DC - 1, tile_position=(0, b * T))
            m.then_inc(x_sc, 1)

        def p_tr(t, p):
            if not valid(t, NT):
                return
            wait(pe, x_plast, t + 1)
            wait(pe, x_pT, t)
            for kc in range(KC):
                pe.transpose(ps[:, 4, kc * P:(kc + 1) * P], prob[:, p, kc * P:(kc + 1) * P], ident)
            pe.transpose(ps[0:BT, 4, KC * P:(KC + 1) * P], p_last[:, p, :], ident).then_inc(x_pt, 1)

        def pv(t, p):
            if not valid(t, NT):
                return
            wait(pe, x_pT, t + 1)
            wait(pe, x_norm, t)
            pe.matmul(ps[:, 5, 0:D], pTl[:, p, :], ctx_l[:, p, :], start=True, stop=False, skip_group_check=True)
            for kc in range(KC):
                for b in range(BT):
                    m = pe.matmul(ps[b * T:(b + 1) * T, 5, 0:D], pT[:, p, kc, b * T:(b + 1) * T], ctx_n[:, p, b, kc, :],
                                  start=False, stop=kc == KC - 1, tile_position=(0, b * T), skip_group_check=True)
            m.then_inc(x_pv, 1)

        def c_tr(t, p):
            if not valid(t, NT):
                return
            wait(pe, x_norm, t + 1)
            wait(pe, x_cT, t)
            for dc in range(DC):
                m = pe.transpose(ps[:, 6, dc * P:(dc + 1) * P], cn[:, dc * P:(dc + 1) * P], ident)
            m.then_inc(x_ct, 1)

        def proj(t, p):
            if not valid(t, NT):
                return
            wait(pe, x_cT, t + 1)
            wait(pe, x_x1, t)
            for dc in range(DC):
                m = pe.matmul(ps[:, 7, 0:D], cT[:, dc, :], w_vo[:, dc, :], start=dc == 0, stop=dc == DC - 1)
            m.then_inc(x_out, 1)

        def xstep(t, p):
            scores(t, p)
            tr(t + 2, p)
            pv(t - 1, 1 - p)
            qk(t + 1, 1 - p)
            p_tr(t, p)
            c_tr(t - 1, 1 - p)
            proj(t - 2, p)

        skewed(pe, xstep, -2, X_LO, X_HI, NT + 2)

        def a_trs(r):
            wait(pe, a_ln, 2 * r + 2)
            wait(pe, a_lo, r)
            for dc in range(DC):
                for s in range(2):
                    m = pe.transpose(ps[:, 4, dc * 2 * P + s * P:dc * 2 * P + (s + 1) * P],
                                     xn2[:, s, dc * P:(dc + 1) * P], ident)
            m.then_inc(a_tr, 1)

        def a_qks(r):
            wait(pe, a_lo, r + 1)
            for n in range(8):
                if n < 4:
                    wait(pe, a_avu, 8 * r + n - 3)
                else:
                    wait(pe, a_qku, 8 * r + n - 3)
                for half in range(2):
                    f = (2 * n + half) * P
                    for dc in range(DC):
                        m = mm3(ps[:, n % 4, half * 2 * P:(half + 1) * 2 * P], wa_hi[:, dc, f:f + P], wa_lo[:, dc, f:f + P],
                                xT_hi[:, dc, :], xT_lo[:, dc, :], dc == 0, dc == DC - 1)
                m.then_inc(a_qk, 1)

        def a_vgs(r):
            for n in range(8):
                s, j = n // 4, n % 4
                wait(pe, a_qku if n < 4 else a_vgu, 8 * r + (n + 5 if n < 4 else n - 3))
                f = 2 * HF + j * 512
                for dc in range(DC):
                    m = mm3(ps[:, n % 4, :], xT_hi[:, dc, s * P:(s + 1) * P], xT_lo[:, dc, s * P:(s + 1) * P],
                            wa_hi[:, dc, f:f + 512], wa_lo[:, dc, f:f + 512], dc == 0, dc == DC - 1)
                m.then_inc(a_vg, 1)

        def a_scores(r):
            for n in range(8):
                s, m4 = n // 4, n % 4
                wait(pe, a_vgu if n < 4 else a_scu, 8 * r + (n + 5 if n < 4 else n - 3))
                for half in range(2):
                    c = 2 * m4 + half
                    m = pe.matmul(ps[:, n % 4, half * 2 * P:(half + 1) * 2 * P], kT[:, c, s * P:(s + 1) * P],
                                  q_pad[:, c, :, s, :], start=True, stop=True)
                m.then_inc(a_sc, 1)

        def a_values(r, s):
            for n in range(4 * s, 4 * s + 4):
                if n < 4:
                    wait(pe, a_scu, 8 * r + n + 5)
                else:
                    wait(pe, a_avu, 8 * r + n - 3)
                    wait(pe, a_scu, 8 * r + 8)
                for q in range(4):
                    h = 4 * (n % 4) + q
                    m = pe.matmul(ps[:, n % 4, q * P:(q + 1) * P], att[:, s, h, :], v_one[:, s, V1 * h:V1 * h + P],
                                  start=True, stop=True)
                m.then_inc(a_av, 1)

        def a_otr(r, s):
            wait(pe, a_avu, 8 * r + 4 * s + 4)
            wait(pe, a_oT, 2 * r + s)
            for c in range(FC):
                m = pe.transpose(ps[:, 5 + c // 4, (c % 4) * P:(c % 4 + 1) * P], o_sb[:, s, c * P:(c + 1) * P], ident)
            m.then_inc(a_ot, 1)

        def a_proj(r, s):
            wait(pe, a_oT, 2 * r + s + 1)
            wait(pe, a_x2, 2 * r + s)
            for c in range(FC):
                m = pe.matmul(ps[:, 7, 0:D], oT[:, c, :], w_out[:, c, :], start=c == 0, stop=c == FC - 1)
            m.then_inc(a_y, 1)

        def astep(r, more=True):
            a_qks(r)
            a_vgs(r)
            a_scores(r)
            a_values(r, 0)
            a_values(r, 1)
            a_otr(r, 0)
            if more:
                a_trs(r + 1)
            a_proj(r, 0)
            a_otr(r, 1)
            a_proj(r, 1)

        a_trs(0)
        pe.wait_ge(s_split_lo, NPIECE)
        pe.wait_ge(l_wo, 32)
        pe.wait_ge(a_init, 2)
        astep(0)
        with pe.Fori(1, NT // 2 - 1) as r:
            astep(r)
        astep(NT // 2 - 1, False)

        def gstep(t, p):
            if valid(t, NT):
                wait(pe, g_ln, t + 1)
                wait(pe, g_xT, t - 1)
                for dc in range(DC):
                    m = pe.transpose(ps[:, p, dc * P:(dc + 1) * P], xn3[:, p, dc * P:(dc + 1) * P], ident)
                m.then_inc(g_tr, 1)
            if valid(t - 1, NT):
                wait(pe, g_xT, t)
                wait(pe, g_sc, t - 2)
                for dc in range(DC):
                    m = pe.matmul(ps[:, 2 + 1 - p, 0:E], xT3[:, 1 - p, dc, :], gw[:, dc, :], start=dc == 0, stop=dc == DC - 1)
                m.then_inc(g_mm, 1)

        skewed(pe, gstep, 0, 4, NT, NT + 1)
        pe.wait_ge(r_sum, 1)
        pe.matmul(ps[:, 4, 0:NT * E], con[:, C_LOW:C_LOW + P], both[:, :, :].rearrange("p t e -> p (t e)"), start=True, stop=True)
        pe.matmul(ps[:, 5, 0:NT * E], ones, both[:, :, :].rearrange("p t e -> p (t e)"), start=True, stop=True).then_inc(r_sum, 1)

        def xtr(t):
            if not valid(t, SLOT_TILES):
                return
            wait(pe, f_xs, 16 * (t + 1))
            wait(pe, f_xT, t)
            for dc in range(DC):
                m = pe.transpose(ps[:, 6, dc * P:(dc + 1) * P], xs_sb[:, dc * P:(dc + 1) * P], ident)
            m.then_inc(f_xtr, 1)

        def up(t):
            if not valid(t, SLOT_TILES):
                return
            e = pe.value_load(tile_e[0:1, bass.ds(t, 1)], min_val=0, max_val=E - 1)
            wait(pe, f_xT, t + 1)
            for j in range(2):
                for w in range(2):
                    if w == 0:
                        wait(pe, f_silu, 2 * t - 1 + j)
                    else:
                        wait(pe, f_h, 2 * t - 1 + j)
                    for dc in range(DC):
                        m = pe.matmul(ps[:, 2 * j + w, :], xT4[:, dc, :],
                                      w13[:, bass.ds(e, 1), w, dc, j * 512:(j + 1) * 512].rearrange("p a n -> p (a n)"),
                                      start=dc == 0, stop=dc == DC - 1)
                    m.then_inc(f_up, 1)

        def down(t):
            if not valid(t, SLOT_TILES):
                return
            wait(pe, f_hT, t + 1)
            wait(pe, f_w2, 16 * (t + 1))
            wait(pe, f_yev, t)
            for c in range(HC):
                m = pe.matmul(ps[:, 7, 0:D], hT[:, c, :], w2_sb[:, c, :], start=c == 0, stop=c == HC - 1)
            m.then_inc(f_y, 1)

        def htr(t):
            if not valid(t, SLOT_TILES):
                return
            wait(pe, f_h, 2 * t + 2)
            wait(pe, f_hT, t)
            for c in range(HC):
                m = pe.transpose(ps[:, 4 + c // 4, (c % 4) * P:(c % 4 + 1) * P], h_sb[:, c * P:(c + 1) * P], ident)
            m.then_inc(f_t, 1)

        def fstep(t):
            up(t)
            xtr(t + 1)
            down(t - 1)
            htr(t)

        pe.wait_ge(l_w13, 16 * (1 + E - EARLY))
        pe.wait_ge(r_map, 1)
        xtr(0)
        for t in range(2):
            fstep(t)
        with pe.Fori(2, SLOT_TILES - 1) as t:
            fstep(t)
        for t in range(SLOT_TILES - 1, SLOT_TILES + 1):
            fstep(t)

    @block.scalar
    def _(act):
        act.wait_ge(s_mm, 1)
        act.activation(m_qk[:, :, :], ps[:, 0, :].rearrange("p (c d) -> p c d", c=DC), ACT.Copy).then_inc(s_ev, 1)
        act.wait_ge(s_mm, 2)
        act.activation(c_qk[:, :], ps[:, 1, 0:DC], ACT.Copy).then_inc(s_ev, 1)
        act.wait_ge(s_mm, 3)
        act.activation(w_vo[:, :, :], ps[:, 2, :].rearrange("p (c d) -> p c d", c=DC), ACT.Copy).then_inc(s_ev, 1)
        act.wait_ge(s_mm, 4)
        act.activation(bias[:, :], ps[:, 3, 0:D], ACT.Copy).then_inc(s_ev, 3)

        def deviation(n):
            act.wait_ge(s_var, n + 1)
            act.activation(rstd[n][:, :], rstd[n][:, :], ACT.Sqrt, bias=eps[:, 0:1]).then_inc(s_sqrt, 1)

        deviation(0)

        def xT_ev(t, p):
            if not valid(t, NT):
                return
            wait(act, x_tr, t + 1)
            wait(act, x_qk, t - 1)
            act.activation(xnT[:, p, :, :], ps[:, 2, 0:D].rearrange("p (c d) -> p c d", c=DC), ACT.Copy).then_inc(x_xnT, 1)

        def qk_ev(t, p):
            if not valid(t, NT):
                return
            wait(act, x_qk, t + 1)
            wait(act, x_sc, t - 1)
            for dc in range(DC):
                m = act.activation(qkT[:, p, dc, :], ps[:, 3, dc * P:(dc + 1) * P], ACT.Identity, bias=c_qk[:, dc:dc + 1])
            m.then_inc(x_qkT, 1)

        def exp(t, p):
            if not valid(t, NT):
                return
            wait(act, x_nmax, t + 1)
            wait(act, x_pt, t - 1)
            act.activation(prob[:, p, 0:S], ps[:, p, 0:S], ACT.Exp, bias=nmx[:, p, :], scale=D ** -0.5,
                           accum_out=rs[:, p, :]).then_inc(x_exp, 1)

        def pT_ev(t, p):
            if not valid(t, NT):
                return
            wait(act, x_pt, t + 1)
            wait(act, x_pv, t - 1)
            act.activation(pT[:, p, :, :], ps[:, 4, 0:KC * P].rearrange("p (c d) -> p c d", c=KC), ACT.Copy)
            act.activation(pTl[:, p, :], ps[0:BT, 4, KC * P:(KC + 1) * P], ACT.Copy).then_inc(x_pT, 1)

        def cT_ev(t, p):
            if not valid(t, NT):
                return
            wait(act, x_ct, t + 1)
            wait(act, x_out, t)
            act.activation(cT[:, :, :], ps[:, 6, 0:D].rearrange("p (c d) -> p c d", c=DC), ACT.Copy).then_inc(x_cT, 1)

        def xstep(t, p):
            xT_ev(t + 2, p)
            exp(t, p)
            qk_ev(t + 1, 1 - p)
            pT_ev(t, p)
            cT_ev(t - 1, 1 - p)

        skewed(act, xstep, -2, X_LO, X_HI, NT + 1)

        deviation(1)

        def a_hi_ev(r):
            wait(act, a_tr, r + 1)
            act.activation(xT_hi[:, :, :], ps[:, 4, :].rearrange("p (c d) -> p c d", c=DC), ACT.Copy).then_inc(a_hi, 1)

        def a_ot_ev(r, s):
            wait(act, a_ot, 2 * r + s + 1)
            wait(act, a_y, 2 * r + s)
            act.activation(oT[:, :, :], ps[:, 5:7, :].rearrange("p a (c d) -> p (a c) d", c=4), ACT.Copy).then_inc(a_oT, 1)

        def astep(r, more=True):
            for n in range(8):
                wait(act, a_qk, 8 * r + n + 1)
                wait(act, a_qku, 8 * r + n - 1)
                act.activation(ex[:, n % 2, :], ps[:, n % 4, :], ACT.Exp).then_inc(a_e, 1)
            for n in range(8):
                s, j = n // 4, n % 4
                wait(act, a_vg, 8 * r + n + 1)
                if j < 2:
                    dst = v_one[:, s, j * 8 * V1:(j + 1) * 8 * V1].rearrange("p (h c) -> p h c", c=V1)[:, :, 0:HD]
                    act.activation(dst, ps[:, n % 4, :].rearrange("p (h c) -> p h c", c=HD), ACT.Copy).then_inc(a_vgu, 1)
                else:
                    act.activation(eg[:, s, (j - 2) * 512:(j - 1) * 512], ps[:, n % 4, :], ACT.Exp, scale=-1.0).then_inc(a_vgu, 1)
            a_ot_ev(r, 0)
            if more:
                a_hi_ev(r + 1)
            a_ot_ev(r, 1)

        a_hi_ev(0)
        act.wait_ge(a_init, 2)
        astep(0)
        with act.Fori(1, NT // 2 - 1) as r:
            astep(r)
        astep(NT // 2 - 1, False)

        deviation(2)

        def gstep(t, p):
            wait(act, g_ln, t + 1)
            act.activation(xn3_all[:, bass.ds(t, 1), :].rearrange("p a d -> p (a d)"), xn3[:, p, :], ACT.Copy).then_inc(g_keep, 1)
            wait(act, g_tr, t + 1)
            wait(act, g_mm, t - 1)
            act.activation(xT3[:, p, :, :], ps[:, p, 0:D].rearrange("p (c d) -> p c d", c=DC), ACT.Copy).then_inc(g_xT, 1)

        skewed(act, gstep, 0, 4, NT, NT)
        act.wait_ge(r_d, 1)
        act.activation(e1[:, :], dv[:, :], ACT.Exp).then_inc(r_e1, 1)

        def xT_evs(t):
            if not valid(t, SLOT_TILES):
                return
            wait(act, f_xtr, t + 1)
            act.activation(xT4[:, :, :], ps[:, 6, 0:D].rearrange("p (c d) -> p c d", c=DC), ACT.Copy).then_inc(f_xT, 1)

        def fstep(t):
            for j in range(2):
                wait(act, f_up, 4 * t + 2 * j + 1)
                wait(act, f_h, 2 * t - 1 + j)
                act.activation(sl[:, j * 512:(j + 1) * 512], ps[:, 2 * j, :], ACT.Silu).then_inc(f_silu, 1)
            xT_evs(t + 1)
            wait(act, f_t, t + 1)
            act.activation(hT[:, :, :], ps[:, 4:6, :].rearrange("p a (c d) -> p (a c) d", c=4), ACT.Copy).then_inc(f_hT, 1)

        xT_evs(0)
        fstep(0)
        with act.Fori(1, SLOT_TILES - 1) as t:
            fstep(t)
        fstep(SLOT_TILES - 1)

    @block.vector
    def _(dve):
        def row(t):
            return x_all[:, bass.ds(t, 1), :].rearrange("p a d -> p (a d)")

        def stats_of(t, n, done):
            dve.bn_stats(bn6[n][:, bass.ds(t, 1), :].rearrange("p a d -> p (a d)"), row(t)).then_inc(done, 1)

        def variance(n, done):
            even, odd = (lambda k: bn6[n][:, :, k]), (lambda k: bn6[n][:, :, 3 + k])
            dve.wait_ge(done, NT)
            dve.tensor_tensor(mean[n][:, :], even(1), odd(1), ALU.add).then_inc(s_part, 1)
            dve.tensor_tensor(half[:, :], even(1), odd(1), ALU.subtract).then_inc(s_part, 1)
            dve.tensor_tensor(rstd[n][:, :], even(2), odd(2), ALU.add).then_inc(s_part, 1)
            dve.wait_ge(s_part, 7 * n + 3)
            dve.tensor_scalar(mean[n][:, :], mean[n][:, :], 0.5, None, ALU.mult).then_inc(s_part, 1)
            dve.tensor_scalar(half[:, :], half[:, :], 0.5, None, ALU.mult).then_inc(s_part, 1)
            dve.wait_ge(s_part, 7 * n + 5)
            dve.tensor_tensor(sq[:, :], half[:, :], half[:, :], ALU.mult).then_inc(s_part, 1)
            dve.tensor_scalar(rstd[n][:, :], rstd[n][:, :], 1.0 / D, None, ALU.mult).then_inc(s_part, 1)
            dve.wait_ge(s_part, 7 * n + 7)
            dve.tensor_tensor(rstd[n][:, :], rstd[n][:, :], sq[:, :], ALU.add).then_inc(s_var, 1)
            dve.wait_ge(s_sqrt, n + 1)
            dve.reciprocal(rstd[n][:, :], rstd[n][:, :]).then_inc(s_rstd, 1)
            dve.wait_ge(s_rstd, n + 1)

        def normed(dst, t, n, done):
            dve.tensor_scalar(dst, row(t), mean[n][:, bass.ds(t, 1)], rstd[n][:, bass.ds(t, 1)],
                              ALU.subtract, ALU.mult).then_inc(done, 1)

        dve.memset(eps[:, :], LN_EPS)
        dve.wait_ge(l_x, 16)
        with dve.Fori(0, NT) as t:
            stats_of(t, 0, s_st)
        dve.wait_ge(l_wx, 16 * 7)
        dve.wait_ge(l_con, 16)
        for ec in range(DC):
            dve.tensor_scalar(bvb[:, ec, :], ones, bvc[:, ec:ec + 1], None, ALU.mult).then_inc(s_bvb, 1)
        variance(0, s_st)

        def ln(t, p):
            if not valid(t, NT):
                return
            wait(dve, x_tr, t - 1)
            normed(xn[:, p, :], t, 0, x_ln)

        def maxes(t, p):
            if not valid(t, NT):
                return
            wait(dve, x_sc, t + 1)
            dve.reduce_max(mx[:, p, :], ps[:, p, 0:S], AX.X).then_inc(x_max, 1)
            dve.wait_ge(x_max, t + 1)
            dve.tensor_scalar(nmx[:, p, :], mx[:, p, :], -(D ** -0.5), None, ALU.mult).then_inc(x_nmax, 1)

        def last_row(t, p):
            if not valid(t, NT):
                return
            wait(dve, x_exp, t + 1)
            dve.reciprocal(rrs[:, p, :], rs[:, p, :])
            dve.tensor_scalar(p_last[:, p, :], con[:, C_BATCH:C_BATCH + BT], prob[:, p, S - 1:S], None,
                              ALU.mult).then_inc(x_plast, 1)

        def norm(t, p):
            if not valid(t, NT):
                return
            wait(dve, x_pv, t + 1)
            wait(dve, x_plast, t + 1)
            wait(dve, x_ct, t)
            dve.tensor_scalar(cn[:, :], ps[:, 5, 0:D], rrs[:, p, :], None, ALU.mult).then_inc(x_norm, 1)

        def x1(t, p):
            if not valid(t, NT):
                return
            wait(dve, x_out, t + 1)
            wait(dve, x_bias, t + 1)
            dve.tensor_tensor(row(t), ps[:, 7, 0:D], row(t), ALU.add).then_inc(x_x1, 1)

        def xstep(t, p):
            maxes(t, p)
            last_row(t, p)
            norm(t - 1, 1 - p)
            x1(t - 2, p)
            if valid(t - 2, NT):
                wait(dve, x_x1, t - 1)
            ln(t + 3, 1 - p)
            if valid(t - 2, NT):
                stats_of(t - 2, 1, x_bn)

        skewed(dve, xstep, -3, X_LO, X_HI, NT + 2)

        variance(1, x_bn)

        def a_lns(r):
            wait(dve, a_tr, r)
            for s in range(2):
                normed(xn2[:, s, :], 2 * r + s, 1, a_ln)

        def a_lo_ev(r):
            wait(dve, a_hi, r + 1)
            dve.tensor_tensor(xT_lo[:, :, :], ps[:, 4, :].rearrange("p (c d) -> p c d", c=DC), xT_hi[:, :, :].bitcast(F32),
                              ALU.subtract).then_inc(a_lo, 1)

        def elus(r):
            for n in range(8):
                if n == 7:
                    wait(dve, a_x2, 2 * r)
                wait(dve, a_e, 8 * r + n + 1)
                dve.tensor_scalar(ex[:, n % 2, :], ex[:, n % 2, :], 1.0, None, ALU.min).then_inc(a_emin, 1)
                dve.wait_ge(a_emin, 8 * r + n + 1)
                if n < 4:
                    for hh in range(2):
                        lo, hi = hh * HD, (hh + 1) * HD
                        m = dve.scalar_tensor_tensor(
                            q_pad[lo:hi, 2 * n:2 * n + 2, hh, :, :].rearrange("p c s t -> p c (s t)"),
                            ps[lo:hi, n % 4, :].rearrange("p (c n) -> p c n", c=2), 0.0,
                            ex[lo:hi, n % 2, :].rearrange("p (c n) -> p c n", c=2), ALU.max, ALU.add)
                else:
                    c = 2 * (n - 4)
                    m = dve.scalar_tensor_tensor(kT[:, c:c + 2, :].rearrange("p c n -> p (c n)"), ps[:, n % 4, :], 0.0,
                                                 ex[:, n % 2, :], ALU.max, ALU.add)
                m.then_inc(a_qku, 1)

        def masks(r):
            mask = con[:, C_MASK:C_MASK + P].rearrange("p (a t) -> p a t", a=1).to_broadcast([P, 4, P])
            for n in range(8):
                s, m4 = n // 4, n % 4
                wait(dve, a_sc, 8 * r + n + 1)
                dve.tensor_tensor(att[:, s, 4 * m4:4 * m4 + 4, :], ps[:, n % 4, :].rearrange("p (h t) -> p h t", h=4),
                                  mask, ALU.mult).then_inc(a_scu, 1)

        def gates(r, s):
            for n in range(4 * s, 4 * s + 4):
                wait(dve, a_av, 8 * r + n + 1)
                num = ps[:, n % 4, :].rearrange("p (h t) -> p h t", h=4)
                g4 = slice((n % 4) * 4 * HD, (n % 4 + 1) * 4 * HD)
                dve.tensor_scalar(dn[:, :, :], num[:, :, HD:V1], DEN_EPS, None, ALU.add).then_inc(a_dn, 1)
                dve.wait_ge(a_dn, 8 * r + n + 1)
                dve.scalar_tensor_tensor(dg[:, :, :], eg[:, s, g4].rearrange("p (h t) -> p h t", h=4), 1.0,
                                         dn[:, :, :].to_broadcast([P, 4, HD]), ALU.add, ALU.mult).then_inc(a_dg, 1)
                dve.wait_ge(a_dg, 8 * r + n + 1)
                dve.reciprocal(rdg[:, :, :], dg[:, :, :]).then_inc(a_rdg, 1)
                dve.wait_ge(a_rdg, 8 * r + n + 1)
                dve.tensor_tensor(o_sb[:, s, g4].rearrange("p (h t) -> p h t", h=4), num[:, :, 0:HD], rdg[:, :, :],
                                  ALU.mult).then_inc(a_avu, 1)

        def x2(r, s):
            t = 2 * r + s
            wait(dve, a_y, t + 1)
            dve.tensor_tensor(row(t), ps[:, 7, 0:D], row(t), ALU.add).then_inc(a_x2, 1)

        def astep(r, more=True):
            elus(r)
            if valid(r - 1, NT):
                for s in range(2):
                    stats_of(2 * (r - 1) + s, 2, a_bn)
            if more:
                a_lns(r + 1)
            masks(r)
            gates(r, 0)
            gates(r, 1)
            if more:
                a_lo_ev(r + 1)
            x2(r, 0)
            x2(r, 1)

        a_lns(0)
        dve.wait_ge(s_split_lo, NPIECE)
        dve.wait_ge(l_z, 16 * (SLOT_TILES * D // ZC))
        dve.memset(q_pad[:, :, :, :, :].rearrange("p c h s t -> p (c h s t)"), 0.0).then_inc(a_init, 1)
        dve.memset(v_one[:, :, :].rearrange("p s w -> p (s w)"), 1.0).then_inc(a_init, 1)
        dve.wait_ge(a_init, 2)
        a_lo_ev(0)
        astep(0)
        with dve.Fori(1, NT // 2 - 1) as r:
            astep(r)
        astep(NT // 2 - 1, False)

        dve.wait_ge(a_x2, NT)
        for s in range(2):
            stats_of(NT - 2 + s, 2, a_bn)
        variance(2, a_bn)

        def g_lns(t, p):
            if not valid(t, NT):
                return
            wait(dve, g_tr, t - 1)
            wait(dve, g_keep, t - 1)
            normed(xn3[:, p, :], t, 2, g_ln)

        def pick(t, p):
            if not valid(t, NT):
                return
            wait(dve, g_mm, t + 1)
            dve.tensor_copy(sc[:, bass.ds(t, 1), :].rearrange("p a n -> p (a n)"), ps[:, 2 + p, 0:E]).then_inc(g_sc, 1)

        def gstep(t, p):
            g_lns(t + 2, p)
            pick(t, p)

        skewed(dve, gstep, -2, 4, NT - 2, NT)
        dve.wait_ge(g_sc, NT)
        for t in range(NT):
            dve.max(m8[:, t, :], sc[:, t, :]).then_inc(g_max, 1)
        dve.wait_ge(g_max, NT)
        for t in range(NT):
            dve.max_index(i8[:, t, :], m8[:, t, :], sc[:, t, :]).then_inc(g_idx, 1)
        dve.wait_ge(g_idx, NT)

        steps = [0]

        def link(m):
            steps[0] += 1
            m.then_inc(r_step, 1)
            dve.wait_ge(r_step, steps[0])

        dve.tensor_tensor(dv[:, :], m8[:, :, 1], m8[:, :, 0], ALU.subtract).then_inc(r_d, 1)
        link(dve.tensor_copy(i8f[:, :, :], i8[:, :, :]))
        iota = con[:, C_IOTA:C_IOTA + E].rearrange("p (a e) -> p a e", a=1).to_broadcast([P, NT, E])
        for k, dst in enumerate((first, second)):
            link(dve.tensor_tensor(dst[:, :, :], i8f[:, :, k:k + 1].to_broadcast([P, NT, E]), iota, ALU.is_equal))
        dve.tensor_tensor(both[:, :, :], first[:, :, :], second[:, :, :], ALU.add).then_inc(r_sum, 1)
        for b in scan:
            link(dve.memset(b[:, 0:8, :], 0.0))
        for b in tiles:
            link(dve.memset(b[:, 0:4], 0.0))
        dve.wait_ge(r_sum, 2)
        link(dve.tensor_copy(scan[0][:, 8:, :], ps[:, 5, 0:NT * E].rearrange("p (t e) -> p t e", e=E)))
        cur = 0
        for d in (1, 2, 4, 8):
            link(dve.tensor_tensor(scan[1 - cur][:, 8:, :], scan[cur][:, 8:, :], scan[cur][:, 8 - d:8 - d + NT, :], ALU.add))
            cur = 1 - cur
        seen = scan[cur]
        total = seen[:, 8 + NT - 1, :]
        link(dve.tensor_tensor(cmp[:, :, :], total.rearrange("p (e a) -> p e a", a=1).to_broadcast([P, E, MAXT]),
                               con[:, C_STEP:C_STEP + MAXT].rearrange("p (a m) -> p a m", a=1).to_broadcast([P, E, MAXT]),
                               ALU.is_gt))
        link(dve.reduce_sum(tiles[0][:, 4:], cmp[:, :, :], AX.X))
        cur = 0
        for d in (1, 2, 4):
            link(dve.tensor_tensor(tiles[1 - cur][:, 4:], tiles[cur][:, 4:], tiles[cur][:, 4 - d:4 - d + E], ALU.add))
            cur = 1 - cur
        end = tiles[cur]
        link(dve.tensor_tensor(slot[:, :, :], ps[:, 4, 0:NT * E].rearrange("p (t e) -> p t e", e=E), seen[:, 7:7 + NT, :], ALU.add))
        link(dve.scalar_tensor_tensor(slot[:, :, :], end[:, 3:3 + E].rearrange("p (a e) -> p a e", a=1).to_broadcast([P, NT, E]),
                                      float(P), slot[:, :, :], ALU.mult, ALU.add))
        for k, chosen in enumerate((first, second)):
            link(dve.tensor_tensor(prod[:, :, :], chosen[:, :, :], slot[:, :, :], ALU.mult))
            link(dve.reduce_sum(posf[:, k, :], prod[:, :, :], AX.X))
        dve.tensor_copy(pos[:, :, :], posf[:, :, :]).then_inc(r_pos, 1)
        link(dve.tensor_tensor(cmp2[:, :, :], con[:, C_TILE:C_TILE + SLOT_TILES].rearrange("p (t a) -> p t a", a=1).to_broadcast([P, SLOT_TILES, E]),
                               end[:, 4:].rearrange("p (a e) -> p a e", a=1).to_broadcast([P, SLOT_TILES, E]), ALU.is_ge))
        link(dve.reduce_sum(tef[:, :], cmp2[:, :, :], AX.X))
        dve.tensor_scalar(tile_e[:, :], tef[:, :], float(E - 1), None, ALU.min).then_inc(r_map, 1)
        dve.wait_ge(r_e1, 1)
        link(dve.tensor_scalar(dv[:, :], e1[:, :], 1.0, None, ALU.add))
        link(dve.reciprocal(top_w[:, 0, :], dv[:, :]))
        link(dve.tensor_tensor(top_w[:, 1, :], e1[:, :], top_w[:, 0, :], ALU.mult))

        def y_ev(t):
            if not valid(t, SLOT_TILES):
                return
            wait(dve, f_y, t + 1)
            wait(dve, f_st, 16 * t)
            dve.tensor_copy(y_sb[:, :], ps[:, 7, 0:D]).then_inc(f_yev, 1)

        def fstep(t):
            if valid(t, SLOT_TILES):
                for j in range(2):
                    wait(dve, f_up, 4 * t + 2 * j + 2)
                    wait(dve, f_silu, 2 * t + j + 1)
                    wait(dve, f_t, t)
                    dve.tensor_tensor(h_sb[:, j * 512:(j + 1) * 512], sl[:, j * 512:(j + 1) * 512], ps[:, 2 * j + 1, :],
                                      ALU.mult).then_inc(f_h, 1)
            y_ev(t - 1)

        for t in range(2):
            fstep(t)
        with dve.Fori(2, SLOT_TILES) as t:
            fstep(t)
        fstep(SLOT_TILES)

        for t in range(NT):
            dve.wait_ge(o_gat[t], 16 * TOP)
            dve.scalar_tensor_tensor(x_all[:, t, :], gat[:, 0, t, :], top_w[:, 0, t:t + 1], x_all[:, t, :],
                                     ALU.mult, ALU.add).then_inc(o_mix, 1)
            dve.wait_ge(o_mix, t + 1)
            dve.scalar_tensor_tensor(x_all[:, t, :], gat[:, 1, t, :], top_w[:, 1, t:t + 1], x_all[:, t, :],
                                     ALU.mult, ALU.add).then_inc(o_sum, 1)


def kernel(x, ctx_1024, L0_xattn_Wk, L0_xattn_Wv, L0_xattn_bv, L0_xattn_Wq, L0_xattn_bq, L0_xattn_Wo, L0_xattn_bo,
           L0_attn_w_qkv, L0_attn_w_gate, L0_attn_w_out, L0_ffn_gate_w, L0_ffn_w1, L0_ffn_w2, L0_ffn_w3):
    import concourse.bacc as bacc
    from concourse.bass_utils import run_bass_kernel_spmd

    ctx4 = np.asarray(ctx_1024).reshape(NT, BT, S, D)
    w1, w3, w2 = (np.asarray(w) for w in (L0_ffn_w1, L0_ffn_w3, L0_ffn_w2))
    arrays = {
        "con": constants(),
        "x": np.asarray(x).reshape(NT, P, D).transpose(1, 0, 2),
        "ctxT": ctx4.transpose(0, 3, 1, 2).reshape(NT, DC, P, BT, S).transpose(0, 2, 3, 1, 4).reshape(NT, P, BT * DC * S),
        "ctxN": ctx4[:, :, :KC * P].reshape(NT, BT, KC, P, D).transpose(0, 3, 1, 2, 4).reshape(NT, P, BT * KC * D),
        "ctxL": ctx4[:, :, S - 1],
        "Wq": np.asarray(L0_xattn_Wq), "Wk": np.asarray(L0_xattn_Wk), "Wv": np.asarray(L0_xattn_Wv),
        "WoT": np.asarray(L0_xattn_Wo).T,
        "bq": np.asarray(L0_xattn_bq).reshape(DC, P).T, "bv": np.asarray(L0_xattn_bv).reshape(DC, P).T,
        "bo": np.asarray(L0_xattn_bo).reshape(1, D),
        "w_a": np.concatenate([np.asarray(L0_attn_w_qkv), np.asarray(L0_attn_w_gate)], axis=1)
                 .reshape(DC, P, 4 * HF).transpose(1, 0, 2).reshape(P, DC * 4 * HF),
        "w_out": np.asarray(L0_attn_w_out),
        "gate": np.asarray(L0_ffn_gate_w).T,
        "w13": np.stack([w1, w3], axis=1).reshape(E, 2, HID, DC, P).transpose(0, 4, 1, 3, 2).reshape(E, P, 2 * DC * HID),
        "w2": w2.reshape(E, D, HC, P).transpose(0, 3, 2, 1).reshape(E, P, HC * D),
    }
    nc = bacc.Bacc("TRN2", target_bir_lowering=False, num_devices=1)
    ins, args = {}, {}
    for name, value in arrays.items():
        value = np.ascontiguousarray(value)
        ins[f"in_{name}"] = value
        args[name] = nc.dram_tensor(f"in_{name}", value.shape, F32, kind="ExternalInput").ap()
    out = nc.dram_tensor("out_x", (P, NT, D), F32, kind="ExternalOutput").ap()
    program(nc, args, out)
    r = run_bass_kernel_spmd(nc, [ins], core_ids=[0])
    return r.results[0]["out_x"].transpose(1, 0, 2).reshape(B, T, D)
```

```python
from contextlib import ExitStack

import numpy as np

import concourse.bass as bass
from concourse import mybir

F32 = mybir.dt.float32
F32R = mybir.dt.float32r
I32 = mybir.dt.int32
U32 = mybir.dt.uint32
ALU = mybir.AluOpType
ACT = mybir.ActivationFunctionType
AX = mybir.AxisListType

P = 128
B, T, D = 64, 32, 256
S = 257
DC = D // P
BT = P // T
NT = B // BT
KC = S // P
H, HD = 16, 64
HF = H * HD
FC = HF // P
E, HID = 8, 1024
HC = HID // P
TOP = 2
SLOT_TILES = (TOP * NT * P + E * (P - 1)) // P
SLOTS = SLOT_TILES * P
MAXT = NT
LN_EPS = 1e-5
DEN_EPS = 1e-6
V1 = HD + 1

C_ID = 0
C_MASK = C_ID + P
C_LOW = C_MASK + P
C_ONES = C_LOW + P
C_BATCH = C_ONES + P
C_IOTA = C_BATCH + BT
C_STEP = C_IOTA + E
C_TILE = C_STEP + MAXT
C_I128 = C_TILE + SLOT_TILES
C_ID1 = C_I128 + P
C_SPARE1 = C_ID1 + NT
C_END = C_SPARE1 + 1


def constants():
    c = np.zeros((P, C_END), np.float32)
    p = np.arange(P)
    c[:, C_ID:C_ID + P] = p[:, None] == p[None, :]
    c[:, C_MASK:C_MASK + P] = (p[:, None] // T == p[None, :] // T) & (p[:, None] <= p[None, :])
    c[:, C_LOW:C_LOW + P] = p[:, None] < p[None, :]
    c[:, C_ONES:C_ONES + P] = 1.0
    c[:, C_BATCH:C_BATCH + BT] = p[:, None] // T == np.arange(BT)[None, :]
    c[:, C_IOTA:C_IOTA + E] = np.arange(E)
    c[:, C_STEP:C_STEP + MAXT] = P * np.arange(MAXT)
    c[:, C_TILE:C_TILE + SLOT_TILES] = np.arange(SLOT_TILES)
    c[:, C_I128:C_I128 + P] = p[None, :]
    c[:, C_ID1:C_ID1 + NT] = p[:, None] + P * np.arange(NT)[None, :] + 1
    c[:, C_SPARE1] = p + NT * P + 1
    return c


def wait(eng, sem, value):
    if isinstance(value, int) and value <= 0:
        return
    eng.wait_ge(sem, value)


def skewed(eng, step, first, lo, hi, last):
    for t in range(first, lo):
        step(t, t % 2)
    with eng.Fori(0, (hi - lo) // 2) as i:
        for u in range(2):
            step(lo + 2 * i + u, (lo + u) % 2)
    for t in range(hi, last):
        step(t, t % 2)


def valid(t, n):
    return not isinstance(t, int) or 0 <= t < n


def program(nc, a, out):
    with ExitStack() as ctx:
        build(nc, ctx, a, out)


def build(nc, ctx, a, out):
    BASE = 16512
    TOP_ADDR = 229344
    EXP_BYTES = 2 * DC * HID * 4
    W13_AT = TOP_ADDR - E * EXP_BYTES
    EARLY = 2
    LATE_AT = W13_AT + EARLY * EXP_BYTES
    slab = ctx.enter_context(nc.sbuf_tensor("slab", [P, (TOP_ADDR - BASE) // 4], F32))
    at = {"low": BASE, "late": LATE_AT}

    def place(name, shape, dtype=F32, where="low"):
        n = 4
        for d in shape[1:]:
            n *= d
        t = nc.alloc_sbuf_tensor_at(name, shape, dtype, offset=at[where])
        at[where] += (n + 31) // 32 * 32
        return t

    con = place("con", [P, C_END])
    bn6 = [place(f"bn6_{i}", [P, NT, 6]) for i in range(3)]
    mean = [place(f"mean{i}", [P, NT]) for i in range(3)]
    rstd = [place(f"rstd{i}", [P, NT]) for i in range(3)]
    half = place("half", [P, NT])
    sq = place("sq", [P, NT])
    eps = place("eps", [P, 1])
    tile_e = place("tile_e", [P, SLOT_TILES], I32)
    slot_row = place("slot_row", [P, SLOT_TILES], I32)
    slot_w = place("slot_w", [P, SLOT_TILES])
    experts_at = at["low"]
    x_all = place("x_all", [P, NT, D])
    gw = place("gw", [P, DC, E])
    w_out = place("w_out", [P, FC, D])
    shared = at["low"]

    w13 = nc.alloc_sbuf_tensor_at("w13", [P, E, 2, DC, HID], F32, offset=W13_AT)
    ident = con[:, C_ID:C_ID + P]
    ones = con[:, C_ONES:C_ONES + P]

    wa_hi = nc.alloc_sbuf_tensor_at("wa_hi", [P, DC, 4 * HF], F32R, offset=TOP_ADDR - 2 * DC * 4 * HF * 4)
    wa_lo = nc.alloc_sbuf_tensor_at("wa_lo", [P, DC, 4 * HF], F32R, offset=TOP_ADDR - DC * 4 * HF * 4)
    SW = 512
    NPIECE = DC * 4 * HF // SW
    assert NPIECE == NT
    wq = place("wq", [P, DC, D], where="late")
    wk = place("wk", [P, DC, D], where="late")
    wv = place("wv", [P, DC, D], where="late")
    wo = place("wo", [P, DC, D], where="late")
    stage = place("stage", [P, 2, SW], where="late")
    ctx_n = place("ctx_n", [P, 2, BT, KC, D], where="late")
    ctx_t = place("ctx_t", [P, 2, BT, DC, S])
    ctx_l = place("ctx_l", [BT, 2, D])
    bqc = place("bqc", [P, DC])
    bvc = place("bvc", [P, DC])
    bor = place("bor", [1, D])
    bvb = place("bvb", [P, DC, P])
    m_qk = place("m_qk", [P, DC, D])
    c_qk = place("c_qk", [P, DC])
    w_vo = place("w_vo", [P, DC, D])
    bias = place("bias", [P, D])
    xn = place("xn", [P, 2, D])
    xnT = place("xnT", [P, 2, DC, P])
    qkT = place("qkT", [P, 2, DC, P])
    mx = place("mx", [P, 2, 1])
    nmx = place("nmx", [P, 2, 1])
    rs = place("rs", [P, 2, 1])
    rrs = place("rrs", [P, 2, 1])
    prob = place("prob", [P, 2, S + 3])
    p_last = place("p_last", [P, 2, BT])
    pT = place("pT", [P, 2, KC, P])
    pTl = place("pTl", [BT, 2, P])
    cn = place("cn", [P, D])
    cT = place("cT", [P, DC, P])
    zero = place("zero", [P, D])
    assert at["low"] <= W13_AT and at["late"] <= TOP_ADDR - 2 * DC * 4 * HF * 4, (at, W13_AT)

    at["low"], at["late"] = shared, LATE_AT
    q_pad = place("q_pad", [P, FC, 2, 2, P], where="late")
    att = place("att", [P, 2, H, P], where="late")
    assert at["late"] <= TOP_ADDR - 2 * DC * 4 * HF * 4
    kT = place("kT", [P, FC, 2 * P])
    xT_hi = place("xT_hi", [P, DC, 2 * P], F32R)
    xT_lo = place("xT_lo", [P, DC, 2 * P], F32R)
    VW = H * V1 + P - V1
    v_one = place("v_one", [P, 2, VW])
    eg = place("eg", [P, 2, HF])
    o_sb = place("o_sb", [P, 2, HF])
    oT = place("oT", [P, FC, P])
    ex = place("ex", [P, 2, 512])
    xn2 = place("xn2", [P, 2, D])
    dn = place("dn", [P, 2, 4, 1])
    rdn = place("rdn", [P, 2, 4, 1])
    gn = place("gn", [P, 2, 4, HD])
    assert at["low"] <= W13_AT, (at, W13_AT)

    PC = 1024
    at["low"] = experts_at + 10 * PC * 4
    at["late"] = LATE_AT
    xn3 = place("xn3", [P, NT, D], where="late")
    assert at["late"] <= LATE_AT + EXP_BYTES
    xT3 = place("xT3", [P, 2, DC, P])
    IN_SLOTS = 4
    sc = place("sc", [P, NT, E])
    m8 = place("m8", [P, NT, 8])
    i8 = place("i8", [P, NT, 8], U32)
    i8f = place("i8f", [P, NT, 8])
    first = place("first", [P, NT, E])
    second = place("second", [P, NT, E])
    both = place("both", [P, NT, E])
    scan = [place(f"scan{i}", [P, NT + 8, E]) for i in range(2)]
    cmp = place("cmp", [P, E, MAXT])
    tiles = [place(f"tiles{i}", [P, 4 + E]) for i in range(2)]
    slot = place("slot", [P, NT, E])
    prod = place("prod", [P, NT, E])
    posf = place("posf", [P, TOP * NT])
    pos = place("pos", [P, TOP * NT], I32)
    pos_tile = place("pos_tile", [P, TOP * NT], I32)
    pos_in = place("pos_in", [P, TOP * NT], I32)
    tilef = place("tilef", [P, TOP * NT])
    inf = place("inf", [P, TOP * NT])
    top_w = place("top_w", [P, TOP, NT])
    cmp2 = place("cmp2", [P, SLOT_TILES, E])
    tef = place("tef", [P, SLOT_TILES])
    dv = place("dv", [P, NT])
    e1 = place("e1", [P, NT])
    in_tile = place("in_tile", [P, TOP * NT, SLOT_TILES])
    what = place("what", [P, TOP * NT, 2, SLOT_TILES])
    in_slot = place("in_slot", [P, IN_SLOTS, 4, P])
    spare = place("spare", [P, SLOT_TILES])
    assert at["low"] <= W13_AT, (at, W13_AT)
    at["low"] = experts_at
    w_hi = place("w_hi", [P, 6, PC], F32R)
    w_lo = place("w_lo", [P, 6, PC], F32R)
    xs_sb = place("xs_sb", [P, D])
    xh = place("xh", [P, DC, P], F32R)
    xl = place("xl", [P, DC, P], F32R)
    h_sb = place("h_sb", [P, HID])
    hh = place("hh", [P, HC, P], F32R)
    hl = place("hl", [P, HC, P], F32R)
    w2_sb = place("w2_sb", [P, HC, D])
    y_sb = place("y_sb", [P, D])
    assert at["low"] <= W13_AT, (at, W13_AT)

    ps = ctx.enter_context(nc.psum_tensor("ps", [P, 8, 512], F32))

    xn_d = nc.dram_tensor("xn_d", ((NT + 1) * P, D), F32, kind="Internal").ap()

    def sem(name):
        return ctx.enter_context(nc.semaphore(name))

    l_con, l_wx, l_wo, l_z = (sem(n) for n in ("l_con", "l_wx", "l_wo", "l_z"))
    XQ = 4
    l_x = [sem(f"l_x{q}") for q in range(XQ)]
    l_stage = [sem("l_stage0"), sem("l_stage1")]
    l_ctxT = [sem("l_ctxT0"), sem("l_ctxT1")]
    l_ctxN = [sem("l_ctxN0"), sem("l_ctxN1")]
    l_w13 = sem("l_w13")
    s_st, s_var, s_part, s_sqrt, s_rstd, s_bvb, s_mm, s_ev, s_zero, s_split_hi, s_split_lo = (
        sem(n) for n in ("s_st", "s_var", "s_part", "s_sqrt", "s_rstd", "s_bvb", "s_mm", "s_ev", "s_zero", "s_split_hi", "s_split_lo"))
    (x_ln, x_tr, x_xnT, x_qk, x_qkT, x_sc, x_max, x_nmax, x_exp, x_plast, x_pt, x_pT, x_pv, x_norm, x_ct, x_cT,
     x_out, x_bias, x_x1, x_bn) = (sem("x_" + n) for n in (
         "ln", "tr", "xnT", "qk", "qkT", "sc", "max", "nmax", "exp", "plast", "pt", "pT", "pv", "norm", "ct", "cT",
         "out", "bias", "x1", "bn"))
    (a_init, a_ln, a_tr, a_hi, a_lo, a_qk, a_e, a_emin, a_qku, a_vg, a_vgu, a_sc, a_scu, a_av, a_dn, a_gn, a_rdn,
     a_avu, a_ot, a_oT, a_y, a_x2, a_bn) = (sem("a_" + n) for n in (
         "init", "ln", "tr", "hi", "lo", "qk", "e", "emin", "qk_used", "vg", "vg_used", "sc", "sc_used", "av", "dn",
         "gn", "rdn", "av_used", "ot", "oT", "y", "x2", "bn"))
    g_ln, g_tr, g_xT, g_mm, g_sc, g_max, g_idx, r_step, r_d, r_e1, r_sum, r_in, r_tab, r_map, r_done = (
        sem(n) for n in ("g_ln", "g_tr", "g_xT", "g_mm", "g_sc", "g_max", "g_idx", "r_step", "r_d", "r_e1",
                         "r_sum", "r_in", "r_tab", "r_map", "r_done"))
    g_keep = sem("g_keep")
    o_init = sem("o_init")
    (f_xs, f_xtr, f_xh, f_xl, f_up, f_dn, f_uhi, f_ulo, f_dhi0, f_dhi1, f_dlo, f_silu, f_h, f_t, f_hh, f_hl, f_y,
     f_st) = (sem("f_" + n) for n in (
         "xs", "xtr", "xh", "xl", "up", "dn", "uhi", "ulo", "dhi0", "dhi1", "dlo", "silu", "h", "t", "hh", "hl",
         "y", "st"))

    f_w2 = [sem("f_w2a"), sem("f_w2b")]

    block = ctx.enter_context(nc.Block())
    X_LO, X_HI = 4, 12

    @block.sync
    def _(sp):
        for buf, name in ((wq, "Wq"), (wk, "Wk"), (wv, "Wv"), (wo, "WoT")):
            sp.dma_start(buf[:, :, :], a[name].rearrange("(c p) n -> p c n", p=P)).then_inc(l_wx, 16)
        for buf, name in ((bqc, "bq"), (bvc, "bv"), (bor, "bo")):
            sp.dma_start(buf[:, :], a[name]).then_inc(l_wx, 16)
        sp.dma_start(con[:, :], a["con"]).then_inc(l_con, 16)
        for q in range(XQ):
            n = NT // XQ
            sp.dma_start(x_all[:, q * n:(q + 1) * n, :], a["x"][:, q * n:(q + 1) * n, :]).then_inc(l_x[q], 16)

        def load(t, p):
            if not valid(t, NT):
                return
            wait(sp, x_sc, t - 1)
            sp.dma_start(ctx_t[:, p, :, :, :].rearrange("p b c s -> p (b c s)"), a["ctxT"][t, :, :]).then_inc(l_ctxT[p], 16)
            wait(sp, x_pv, t - 1)
            sp.dma_start(ctx_n[:, p, :, :, :].rearrange("p b c d -> p (b c d)"), a["ctxN"][t, :, :]).then_inc(l_ctxN[p], 16)
            sp.dma_start(ctx_l[:, p, :], a["ctxL"][t, :, :]).then_inc(l_ctxN[p], 16)
            wait(sp, s_split_lo, t - 1)
            sp.dma_start(stage[:, p, :], a["w_a"][:, bass.ds(t * SW, SW)]).then_inc(l_stage[p], 16)

        for t in range(2):
            load(t, t)
        sp.dma_start(w_out[:, :, :], a["w_out"].rearrange("(c p) n -> p c n", p=P)).then_inc(l_wo, 16)
        sp.dma_start(gw[:, :, :], a["gate"].rearrange("(c p) n -> p c n", p=P)).then_inc(l_wo, 16)
        for t in range(2, X_LO):
            load(t, t % 2)
        with sp.Fori(0, (X_HI - X_LO) // 2) as i:
            for u in range(2):
                load(X_LO + 2 * i + u, u)
        for t in range(X_HI, NT):
            load(t, t % 2)
        def load_expert(e):
            sp.dma_start(w13[:, e, :, :, :].rearrange("p w c h -> p (w c h)"), a["w13"][e, :, :]).then_inc(l_w13, 16)

        for e in range(EARLY):
            load_expert(e)
        sp.wait_ge(a_vg, 8 * NT // 2)
        for e in range(E // 2, E):
            load_expert(e)
        sp.wait_ge(a_av, 8 * NT // 2)
        for e in range(EARLY + 1, E // 2):
            load_expert(e)
        sp.wait_ge(a_x2, NT)
        sp.dma_start(out[0:NT * P, :].rearrange("(t p) d -> p t d", p=P), x_all[:, :, :]).then_inc(o_init, 16)
        for q in range(XQ):
            sp.wait_ge(g_ln, (q + 1) * NT // XQ)
            ts = slice(q * NT // XQ, (q + 1) * NT // XQ)
            sp.dma_start(xn_d[ts.start * P:ts.stop * P, :].rearrange("(t p) d -> p t d", p=P), xn3[:, ts, :]).then_inc(g_keep, 16)
        sp.wait_ge(g_keep, 16 * XQ)
        sp.wait_ge(g_tr, NT)
        load_expert(EARLY)

        def load_w2(t):
            e = sp.value_load(tile_e[0:1, bass.ds(t, 1)], min_val=0, max_val=E - 1)
            for c in range(2):
                wait(sp, f_dlo, 2 * (t - 1) + c + 1)
                sp.dma_start(w2_sb[:, c * HC // 2:(c + 1) * HC // 2, :].rearrange("p c d -> p (c d)"),
                             a["w2"][bass.ds(e, 1), :, c * HC // 2 * D:(c + 1) * HC // 2 * D].rearrange("e p n -> (e p) n")).then_inc(f_w2[c], 16)

        sp.wait_ge(r_done, 1)
        load_w2(0)
        with sp.Fori(1, SLOT_TILES) as t:
            load_w2(t)
        sp.wait_ge(f_st, 16 * SLOT_TILES)

    @block.gpsimd
    def _(pool):
        pool.memset(zero[:, :], 0.0).then_inc(s_zero, 1)
        pool.wait_ge(s_zero, 1)
        pool.dma_start(xn_d[NT * P:, :], zero[:, :]).then_inc(l_z, 16)
        pool.dma_start(out[NT * P:, :], zero[:, :]).then_inc(l_z, 16)
        pool.wait_ge(s_ev, 6)
        hi_all = wa_hi[:, :, :].rearrange("p c n -> p (c n)")
        lo_all = wa_lo[:, :, :].rearrange("p c n -> p (c n)")
        with pool.Fori(0, NT // 2) as i:
            for p in range(2):
                t = 2 * i + p
                pool.wait_ge(x_ln, t + 1)
                row = x_all[:, bass.ds(t, 1), :].rearrange("p a d -> p (a d)")
                pool.tensor_tensor(row, row, bias[:, :], ALU.add).then_inc(x_bias, 1)
                pool.wait_ge(l_stage[p], 16 * i + 16)
                pool.tensor_copy(hi_all[:, bass.ds(t * SW, SW)], stage[:, p, :]).then_inc(s_split_hi, 1)
                pool.wait_ge(s_split_hi, t + 1)
                pool.tensor_tensor(lo_all[:, bass.ds(t * SW, SW)], stage[:, p, :],
                                   hi_all[:, bass.ds(t * SW, SW)].bitcast(F32), ALU.subtract).then_inc(s_split_lo, 1)
        def gather(t):
            if not valid(t, SLOT_TILES):
                return
            wait(pool, f_xtr, t)
            pool.indirect_dma_start(xs_sb[:, :], None, xn_d, bass.IndirectOffsetOnAxis(slot_row[:, t:t + 1], 0)).then_inc(f_xs, 16)

        def low(t):
            for c in range(2):
                pool.wait_ge((f_dhi0, f_dhi1)[c], t + 1)
                src = w2_sb[:, c * HC // 2:(c + 1) * HC // 2, :].rearrange("p c d -> p (c d)")
                pool.tensor_tensor(w_lo[:, 4 + c, :], src, w_hi[:, 4 + c, :].bitcast(F32), ALU.subtract).then_inc(f_dlo, 1)

        pool.wait_ge(l_z, 32)
        pool.wait_ge(o_init, 16)
        pool.wait_ge(r_done, 1)
        pool.wait_ge(g_keep, 16 * XQ)
        def scatter(t):
            if not valid(t, SLOT_TILES):
                return
            pool.wait_ge(f_y, t + 1)
            wait(pool, f_st, 16 * t)
            pool.indirect_dma_start(out, bass.IndirectOffsetOnAxis(slot_row[:, t:t + 1], 0), y_sb[:, :], None,
                                    compute_op=ALU.add).then_inc(f_st, 16)

        gather(0)
        gather(1)
        for t in range(SLOT_TILES + 1):
            gather(t + 2)
            if t < SLOT_TILES:
                low(t)
            scatter(t - 1)

    @block.tensor
    def _(pe):
        def mm3(dst, l_hi, l_lo, r_hi, r_lo, first, last):
            pe.matmul(dst, l_hi, r_hi, start=first, stop=False)
            pe.matmul(dst, l_hi, r_lo, start=False, stop=False)
            return pe.matmul(dst, l_lo, r_hi, start=False, stop=last)

        pe.wait_ge(l_wx, 16 * 7)
        pe.wait_ge(l_con, 16)
        for dc in range(DC):
            for ec in range(DC):
                m = pe.matmul(ps[:, 0, dc * D:(dc + 1) * D], wq[:, ec, dc * P:(dc + 1) * P], wk[:, ec, :],
                              start=ec == 0, stop=ec == DC - 1)
        m.then_inc(s_mm, 1)
        for dc in range(DC):
            for ec in range(DC):
                m = pe.matmul(ps[:, 1, dc:dc + 1], wk[:, ec, dc * P:(dc + 1) * P], bqc[:, ec:ec + 1],
                              start=ec == 0, stop=ec == DC - 1)
        m.then_inc(s_mm, 1)
        for dc in range(DC):
            for ec in range(DC):
                m = pe.matmul(ps[:, 2, dc * D:(dc + 1) * D], wv[:, ec, dc * P:(dc + 1) * P], wo[:, ec, :],
                              start=ec == 0, stop=ec == DC - 1)
        m.then_inc(s_mm, 1)
        pe.wait_ge(s_bvb, DC)
        for ec in range(DC):
            pe.matmul(ps[:, 3, 0:D], bvb[:, ec, :], wo[:, ec, :], start=ec == 0, stop=False)
        pe.matmul(ps[:, 3, 0:D], ones[0:1, :], bor[0:1, :], start=False, stop=True).then_inc(s_mm, 1)
        pe.wait_ge(s_ev, 6)

        def tr(t, p):
            if not valid(t, NT):
                return
            wait(pe, x_ln, t + 1)
            wait(pe, x_xnT, t)
            for dc in range(DC):
                m = pe.transpose(ps[:, 2, dc * P:(dc + 1) * P], xn[:, p, dc * P:(dc + 1) * P], ident)
            m.then_inc(x_tr, 1)

        def qk(t, p):
            if not valid(t, NT):
                return
            wait(pe, x_xnT, t + 1)
            wait(pe, x_qkT, t)
            for oc in range(DC):
                for dc in range(DC):
                    m = pe.matmul(ps[:, 3, oc * P:(oc + 1) * P], m_qk[:, dc, oc * P:(oc + 1) * P], xnT[:, p, dc, :],
                                  start=dc == 0, stop=dc == DC - 1)
            m.then_inc(x_qk, 1)

        def scores(t, p):
            if not valid(t, NT):
                return
            pe.wait_ge(l_ctxT[p], 8 * (t - p) + 16)
            wait(pe, x_qkT, t + 1)
            wait(pe, x_exp, t - 1)
            for dc in range(DC):
                for b in range(BT):
                    m = pe.matmul(ps[b * T:(b + 1) * T, p, 0:S], qkT[:, p, dc, b * T:(b + 1) * T], ctx_t[:, p, b, dc, :],
                                  start=dc == 0, stop=dc == DC - 1, tile_position=(0, b * T))
            m.then_inc(x_sc, 1)

        def p_tr(t, p):
            if not valid(t, NT):
                return
            wait(pe, x_plast, t + 1)
            wait(pe, x_pT, t)
            for kc in range(KC):
                pe.transpose(ps[:, 4, kc * P:(kc + 1) * P], prob[:, p, kc * P:(kc + 1) * P], ident)
            pe.transpose(ps[0:BT, 4, KC * P:(KC + 1) * P], p_last[:, p, :], ident).then_inc(x_pt, 1)

        def pv(t, p):
            if not valid(t, NT):
                return
            wait(pe, x_pT, t + 1)
            wait(pe, x_norm, t)
            pe.wait_ge(l_ctxN[p], 16 * (t - p) + 32)
            pe.matmul(ps[:, 5, 0:D], pTl[:, p, :], ctx_l[:, p, :], start=True, stop=False, skip_group_check=True)
            for kc in range(KC):
                for b in range(BT):
                    m = pe.matmul(ps[b * T:(b + 1) * T, 5, 0:D], pT[:, p, kc, b * T:(b + 1) * T], ctx_n[:, p, b, kc, :],
                                  start=False, stop=kc == KC - 1, tile_position=(0, b * T), skip_group_check=True)
            m.then_inc(x_pv, 1)

        def c_tr(t, p):
            if not valid(t, NT):
                return
            wait(pe, x_norm, t + 1)
            wait(pe, x_cT, t)
            for dc in range(DC):
                m = pe.transpose(ps[:, 6, dc * P:(dc + 1) * P], cn[:, dc * P:(dc + 1) * P], ident)
            m.then_inc(x_ct, 1)

        def proj(t, p):
            if not valid(t, NT):
                return
            wait(pe, x_cT, t + 1)
            wait(pe, x_x1, t)
            for dc in range(DC):
                m = pe.matmul(ps[:, 7, 0:D], cT[:, dc, :], w_vo[:, dc, :], start=dc == 0, stop=dc == DC - 1)
            m.then_inc(x_out, 1)

        def xstep(t, p):
            scores(t, p)
            tr(t + 2, p)
            pv(t - 1, 1 - p)
            qk(t + 1, 1 - p)
            p_tr(t, p)
            c_tr(t - 1, 1 - p)
            proj(t - 2, p)

        skewed(pe, xstep, -2, X_LO, X_HI, NT + 2)

        def a_trs(r):
            wait(pe, a_ln, 2 * r + 2)
            wait(pe, a_lo, r)
            for dc in range(DC):
                for s in range(2):
                    m = pe.transpose(ps[:, 4, dc * 2 * P + s * P:dc * 2 * P + (s + 1) * P],
                                     xn2[:, s, dc * P:(dc + 1) * P], ident)
            m.then_inc(a_tr, 1)

        def a_qks(r):
            wait(pe, a_lo, r + 1)
            for n in range(8):
                if n < 4:
                    wait(pe, a_avu, 8 * r + n - 3)
                else:
                    wait(pe, a_qku, 8 * r + n - 3)
                for half in range(2):
                    f = (2 * n + half) * P
                    for dc in range(DC):
                        m = mm3(ps[:, n % 4, half * 2 * P:(half + 1) * 2 * P], wa_hi[:, dc, f:f + P], wa_lo[:, dc, f:f + P],
                                xT_hi[:, dc, :], xT_lo[:, dc, :], dc == 0, dc == DC - 1)
                m.then_inc(a_qk, 1)

        def a_vgs(r):
            for n in range(8):
                s, j = n // 4, n % 4
                wait(pe, a_qku if n < 4 else a_vgu, 8 * r + (n + 5 if n < 4 else n - 3))
                f = 2 * HF + j * 512
                for dc in range(DC):
                    m = mm3(ps[:, n % 4, :], xT_hi[:, dc, s * P:(s + 1) * P], xT_lo[:, dc, s * P:(s + 1) * P],
                            wa_hi[:, dc, f:f + 512], wa_lo[:, dc, f:f + 512], dc == 0, dc == DC - 1)
                m.then_inc(a_vg, 1)

        def a_scores(r):
            for n in range(8):
                s, m4 = n // 4, n % 4
                wait(pe, a_vgu if n < 4 else a_scu, 8 * r + (n + 5 if n < 4 else n - 3))
                for half in range(2):
                    c = 2 * m4 + half
                    m = pe.matmul(ps[:, n % 4, half * 2 * P:(half + 1) * 2 * P], kT[:, c, s * P:(s + 1) * P],
                                  q_pad[:, c, :, s, :], start=True, stop=True)
                m.then_inc(a_sc, 1)

        def a_values(r, s):
            for n in range(4 * s, 4 * s + 4):
                if n < 4:
                    wait(pe, a_scu, 8 * r + n + 5)
                else:
                    wait(pe, a_avu, 8 * r + n - 3)
                    wait(pe, a_scu, 8 * r + 8)
                for q in range(4):
                    h = 4 * (n % 4) + q
                    m = pe.matmul(ps[:, n % 4, q * P:(q + 1) * P], att[:, s, h, :], v_one[:, s, V1 * h:V1 * h + P],
                                  start=True, stop=True)
                m.then_inc(a_av, 1)

        def a_otr(r, s):
            wait(pe, a_avu, 8 * r + 4 * s + 4)
            wait(pe, a_oT, 2 * r + s)
            for c in range(FC):
                m = pe.transpose(ps[:, 5 + c // 4, (c % 4) * P:(c % 4 + 1) * P], o_sb[:, s, c * P:(c + 1) * P], ident)
            m.then_inc(a_ot, 1)

        def a_proj(r, s):
            wait(pe, a_oT, 2 * r + s + 1)
            wait(pe, a_x2, 2 * r + s)
            for c in range(FC):
                m = pe.matmul(ps[:, 7, 0:D], oT[:, c, :], w_out[:, c, :], start=c == 0, stop=c == FC - 1)
            m.then_inc(a_y, 1)

        def astep(r, more=True):
            a_qks(r)
            a_vgs(r)
            a_scores(r)
            a_values(r, 0)
            a_values(r, 1)
            a_otr(r, 0)
            if more:
                a_trs(r + 1)
            a_proj(r, 0)
            a_otr(r, 1)
            a_proj(r, 1)

        a_trs(0)
        pe.wait_ge(s_split_lo, NPIECE)
        pe.wait_ge(l_wo, 32)
        pe.wait_ge(a_init, 2)
        astep(0)
        with pe.Fori(1, NT // 2 - 1) as r:
            astep(r)
        astep(NT // 2 - 1, False)

        def gstep(t, p):
            if valid(t, NT):
                wait(pe, g_ln, t + 1)
                wait(pe, g_xT, t - 1)
                for dc in range(DC):
                    m = pe.transpose(ps[:, p, dc * P:(dc + 1) * P],
                                     xn3[:, t, dc * P:(dc + 1) * P], ident)
                m.then_inc(g_tr, 1)
            if valid(t - 1, NT):
                wait(pe, g_xT, t)
                wait(pe, g_sc, t - 2)
                for dc in range(DC):
                    m = pe.matmul(ps[:, 2 + 1 - p, 0:E], xT3[:, 1 - p, dc, :], gw[:, dc, :], start=dc == 0, stop=dc == DC - 1)
                m.then_inc(g_mm, 1)

        for t in range(NT + 1):
            gstep(t, t % 2)
        pe.wait_ge(r_sum, 1)
        pe.matmul(ps[:, 4, 0:NT * E], con[:, C_LOW:C_LOW + P], both[:, :, :].rearrange("p t e -> p (t e)"), start=True, stop=True)
        pe.matmul(ps[:, 5, 0:NT * E], ones, both[:, :, :].rearrange("p t e -> p (t e)"), start=True, stop=True).then_inc(r_sum, 1)

        for q in range(TOP * NT // 4):
            pe.wait_ge(r_in, q + 1)
            for k in range(4):
                n = 4 * q + k
                m = pe.matmul(ps[:, 6, 0:2 * SLOT_TILES], in_slot[:, q % IN_SLOTS, k, :], what[:, n, :, :].rearrange("p a t -> p (a t)"),
                              start=n == 0, stop=n == TOP * NT - 1)
            m.then_inc(r_tab, 1)

        def xtr(t):
            if not valid(t, SLOT_TILES):
                return
            wait(pe, f_xs, 16 * (t + 1))
            wait(pe, f_xl, t)
            for dc in range(DC):
                m = pe.transpose(ps[:, 6, dc * P:(dc + 1) * P], xs_sb[:, dc * P:(dc + 1) * P], ident)
            m.then_inc(f_xtr, 1)

        def up(t):
            if not valid(t, SLOT_TILES):
                return
            wait(pe, f_xl, t + 1)
            for c in range(4):
                wait(pe, f_silu if c % 2 == 0 else f_h, 2 * t - 1 + c // 2)
                wait(pe, f_ulo, 4 * t + c + 1)
                for dc in range(DC):
                    cols = slice(dc * 512, (dc + 1) * 512)
                    m = mm3(ps[:, c, :], xh[:, dc, :], xl[:, dc, :], w_hi[:, c, cols], w_lo[:, c, cols],
                            dc == 0, dc == DC - 1)
                m.then_inc(f_up, 1)

        def down(t):
            if not valid(t, SLOT_TILES):
                return
            wait(pe, f_hl, t + 1)
            wait(pe, f_y, t)
            for c in range(HC):
                half_ = c // (HC // 2)
                if c % (HC // 2) == 0:
                    wait(pe, f_dlo, 2 * t + half_ + 1)
                cols = slice(c % (HC // 2) * D, (c % (HC // 2) + 1) * D)
                m = mm3(ps[:, 7, 0:D], hh[:, c, :], hl[:, c, :], w_hi[:, 4 + half_, cols], w_lo[:, 4 + half_, cols],
                        c == 0, c == HC - 1)
                if c % (HC // 2) == HC // 2 - 1:
                    m.then_inc(f_dn, 1)

        def htr(t):
            if not valid(t, SLOT_TILES):
                return
            wait(pe, f_h, 2 * t + 2)
            wait(pe, f_hl, t)
            for c in range(HC):
                m = pe.transpose(ps[:, 4 + c // 4, (c % 4) * P:(c % 4 + 1) * P], h_sb[:, c * P:(c + 1) * P], ident)
            m.then_inc(f_t, 1)

        def fstep(t):
            up(t)
            xtr(t + 1)
            down(t - 1)
            htr(t)

        xtr(0)
        for t in range(2):
            fstep(t)
        with pe.Fori(2, SLOT_TILES - 1) as t:
            fstep(t)
        for t in range(SLOT_TILES - 1, SLOT_TILES + 1):
            fstep(t)

    @block.scalar
    def _(act):
        act.wait_ge(s_mm, 1)
        act.activation(m_qk[:, :, :], ps[:, 0, :].rearrange("p (c d) -> p c d", c=DC), ACT.Copy).then_inc(s_ev, 1)
        act.wait_ge(s_mm, 2)
        act.activation(c_qk[:, :], ps[:, 1, 0:DC], ACT.Copy).then_inc(s_ev, 1)
        act.wait_ge(s_mm, 3)
        act.activation(w_vo[:, :, :], ps[:, 2, :].rearrange("p (c d) -> p c d", c=DC), ACT.Copy).then_inc(s_ev, 1)
        act.wait_ge(s_mm, 4)
        act.activation(bias[:, :], ps[:, 3, 0:D], ACT.Copy).then_inc(s_ev, 3)

        def deviation(n):
            act.wait_ge(s_var, n + 1)
            act.activation(rstd[n][:, :], rstd[n][:, :], ACT.Sqrt, bias=eps[:, 0:1]).then_inc(s_sqrt, 1)

        deviation(0)

        def xT_ev(t, p):
            if not valid(t, NT):
                return
            wait(act, x_tr, t + 1)
            wait(act, x_qk, t - 1)
            act.activation(xnT[:, p, :, :], ps[:, 2, 0:D].rearrange("p (c d) -> p c d", c=DC), ACT.Copy).then_inc(x_xnT, 1)

        def qk_ev(t, p):
            if not valid(t, NT):
                return
            wait(act, x_qk, t + 1)
            wait(act, x_sc, t - 1)
            for dc in range(DC):
                m = act.activation(qkT[:, p, dc, :], ps[:, 3, dc * P:(dc + 1) * P], ACT.Identity, bias=c_qk[:, dc:dc + 1])
            m.then_inc(x_qkT, 1)

        def exp(t, p):
            if not valid(t, NT):
                return
            wait(act, x_nmax, t + 1)
            wait(act, x_pt, t - 1)
            act.activation(prob[:, p, 0:S], ps[:, p, 0:S], ACT.Exp, bias=nmx[:, p, :], scale=D ** -0.5,
                           accum_out=rs[:, p, :]).then_inc(x_exp, 1)

        def pT_ev(t, p):
            if not valid(t, NT):
                return
            wait(act, x_pt, t + 1)
            wait(act, x_pv, t - 1)
            act.activation(pT[:, p, :, :], ps[:, 4, 0:KC * P].rearrange("p (c d) -> p c d", c=KC), ACT.Copy)
            act.activation(pTl[:, p, :], ps[0:BT, 4, KC * P:(KC + 1) * P], ACT.Copy).then_inc(x_pT, 1)

        def cT_ev(t, p):
            if not valid(t, NT):
                return
            wait(act, x_ct, t + 1)
            wait(act, x_out, t)
            act.activation(cT[:, :, :], ps[:, 6, 0:D].rearrange("p (c d) -> p c d", c=DC), ACT.Copy).then_inc(x_cT, 1)

        def xstep(t, p):
            xT_ev(t + 2, p)
            exp(t, p)
            qk_ev(t + 1, 1 - p)
            pT_ev(t, p)
            cT_ev(t - 1, 1 - p)

        skewed(act, xstep, -2, X_LO, X_HI, NT + 1)

        deviation(1)

        def a_hi_ev(r):
            wait(act, a_tr, r + 1)
            act.activation(xT_hi[:, :, :], ps[:, 4, :].rearrange("p (c d) -> p c d", c=DC), ACT.Copy).then_inc(a_hi, 1)

        def a_ot_ev(r, s):
            wait(act, a_ot, 2 * r + s + 1)
            wait(act, a_y, 2 * r + s)
            act.activation(oT[:, :, :], ps[:, 5:7, :].rearrange("p a (c d) -> p (a c) d", c=4), ACT.Copy).then_inc(a_oT, 1)

        def astep(r, more=True):
            for n in range(8):
                wait(act, a_qk, 8 * r + n + 1)
                wait(act, a_qku, 8 * r + n - 1)
                act.activation(ex[:, n % 2, :], ps[:, n % 4, :], ACT.Exp).then_inc(a_e, 1)
            for n in range(8):
                s, j = n // 4, n % 4
                wait(act, a_vg, 8 * r + n + 1)
                if j < 2:
                    dst = v_one[:, s, j * 8 * V1:(j + 1) * 8 * V1].rearrange("p (h c) -> p h c", c=V1)[:, :, 0:HD]
                    act.activation(dst, ps[:, n % 4, :].rearrange("p (h c) -> p h c", c=HD), ACT.Copy).then_inc(a_vgu, 1)
                else:
                    act.activation(eg[:, s, (j - 2) * 512:(j - 1) * 512], ps[:, n % 4, :], ACT.Sigmoid).then_inc(a_vgu, 1)
            a_ot_ev(r, 0)
            if more:
                a_hi_ev(r + 1)
            a_ot_ev(r, 1)

        a_hi_ev(0)
        act.wait_ge(a_init, 2)
        astep(0)
        with act.Fori(1, NT // 2 - 1) as r:
            astep(r)
        astep(NT // 2 - 1, False)

        deviation(2)

        def gstep(t, p):
            wait(act, g_tr, t + 1)
            wait(act, g_mm, t - 1)
            act.activation(xT3[:, p, :, :], ps[:, p, 0:D].rearrange("p (c d) -> p c d", c=DC), ACT.Copy).then_inc(g_xT, 1)

        skewed(act, gstep, 0, 4, NT, NT)
        act.wait_ge(r_d, 1)
        act.activation(e1[:, :], dv[:, :], ACT.Exp).then_inc(r_e1, 1)

        def up_hi(t, cs, e):
            if not valid(t, SLOT_TILES):
                return
            for c in cs:
                wait(act, f_up, 4 * (t - 1) + c + 1)
                act.activation(w_hi[:, c, :].rearrange("p (c n) -> p c n", c=DC),
                               w13[:, bass.ds(e, 1), c % 2, :, c // 2 * 512:(c // 2 + 1) * 512].rearrange("p a c n -> p (a c) n"),
                               ACT.Copy).then_inc(f_uhi, 1)

        def down_hi(t):
            if not valid(t, SLOT_TILES):
                return
            wait(act, f_w2[0], 16 * (t + 1))
            wait(act, f_dn, 2 * (t - 1) + 1)
            act.activation(w_hi[:, 4, :], w2_sb[:, 0:HC // 2, :].rearrange("p c d -> p (c d)"), ACT.Copy).then_inc(f_dhi0, 1)

        def silu(t, j):
            if not valid(t, SLOT_TILES):
                return
            wait(act, f_up, 4 * t + 2 * j + 1)
            wait(act, f_t, t)
            act.activation(h_sb[:, j * 512:(j + 1) * 512], ps[:, 2 * j, :], ACT.Silu).then_inc(f_silu, 1)

        def x_hi(t):
            if not valid(t, SLOT_TILES):
                return
            wait(act, f_xtr, t + 1)
            wait(act, f_up, 4 * t)
            act.activation(xh[:, :, :], ps[:, 6, 0:D].rearrange("p (c d) -> p c d", c=DC), ACT.Copy).then_inc(f_xh, 1)

        def y_ev(t):
            if not valid(t, SLOT_TILES):
                return
            wait(act, f_dn, 2 * t + 2)
            wait(act, f_st, 16 * t)
            act.activation(y_sb[:, :], ps[:, 7, 0:D], ACT.Identity, scale=slot_w[:, bass.ds(t, 1)]).then_inc(f_y, 1)

        def h_hi(t):
            if not valid(t, SLOT_TILES):
                return
            wait(act, f_t, t + 1)
            act.activation(hh[:, :, :], ps[:, 4:6, :].rearrange("p a (c d) -> p (a c) d", c=4), ACT.Copy).then_inc(f_hh, 1)

        def expert(t):
            return act.value_load(tile_e[0:1, bass.ds(t, 1)], min_val=0, max_val=E - 1) if valid(t, SLOT_TILES) else None

        def fstep(t):
            e = expert(t + 1)
            silu(t, 0)
            up_hi(t + 1, (0, 1), e)
            silu(t, 1)
            up_hi(t + 1, (2,), e)
            x_hi(t + 1)
            up_hi(t + 1, (3,), e)
            down_hi(t)
            y_ev(t - 1)
            h_hi(t)

        act.wait_ge(o_init, 16)
        act.wait_ge(r_map, 1)
        act.wait_ge(l_w13, 16 * E)
        up_hi(0, range(4), expert(0))
        x_hi(0)
        for t in range(2):
            fstep(t)
        with act.Fori(2, SLOT_TILES - 1) as t:
            fstep(t)
        for t in range(SLOT_TILES - 1, SLOT_TILES + 1):
            fstep(t)

    @block.vector
    def _(dve):
        def row(t):
            return x_all[:, bass.ds(t, 1), :].rearrange("p a d -> p (a d)")

        def stats_of(t, n, done):
            dve.bn_stats(bn6[n][:, bass.ds(t, 1), :].rearrange("p a d -> p (a d)"), row(t)).then_inc(done, 1)

        def variance(n, done):
            even, odd = (lambda k: bn6[n][:, :, k]), (lambda k: bn6[n][:, :, 3 + k])
            dve.wait_ge(done, NT)
            dve.tensor_tensor(mean[n][:, :], even(1), odd(1), ALU.add).then_inc(s_part, 1)
            dve.tensor_tensor(half[:, :], even(1), odd(1), ALU.subtract).then_inc(s_part, 1)
            dve.tensor_tensor(rstd[n][:, :], even(2), odd(2), ALU.add).then_inc(s_part, 1)
            dve.wait_ge(s_part, 7 * n + 3)
            dve.tensor_scalar(mean[n][:, :], mean[n][:, :], 0.5, None, ALU.mult).then_inc(s_part, 1)
            dve.tensor_scalar(half[:, :], half[:, :], 0.5, None, ALU.mult).then_inc(s_part, 1)
            dve.wait_ge(s_part, 7 * n + 5)
            dve.tensor_tensor(sq[:, :], half[:, :], half[:, :], ALU.mult).then_inc(s_part, 1)
            dve.tensor_scalar(rstd[n][:, :], rstd[n][:, :], 1.0 / D, None, ALU.mult).then_inc(s_part, 1)
            dve.wait_ge(s_part, 7 * n + 7)
            dve.tensor_tensor(rstd[n][:, :], rstd[n][:, :], sq[:, :], ALU.add).then_inc(s_var, 1)
            dve.wait_ge(s_sqrt, n + 1)
            dve.reciprocal(rstd[n][:, :], rstd[n][:, :]).then_inc(s_rstd, 1)
            dve.wait_ge(s_rstd, n + 1)

        def normed(dst, t, n, done):
            dve.tensor_scalar(dst, row(t), mean[n][:, bass.ds(t, 1)], rstd[n][:, bass.ds(t, 1)],
                              ALU.subtract, ALU.mult).then_inc(done, 1)

        dve.memset(eps[:, :], LN_EPS)
        for q in range(XQ):
            dve.wait_ge(l_x[q], 16)
            for t in range(q * NT // XQ, (q + 1) * NT // XQ):
                stats_of(t, 0, s_st)
        dve.wait_ge(l_wx, 16 * 7)
        dve.wait_ge(l_con, 16)
        for ec in range(DC):
            dve.tensor_scalar(bvb[:, ec, :], ones, bvc[:, ec:ec + 1], None, ALU.mult).then_inc(s_bvb, 1)
        variance(0, s_st)

        def ln(t, p):
            if not valid(t, NT):
                return
            wait(dve, x_tr, t - 1)
            normed(xn[:, p, :], t, 0, x_ln)

        def maxes(t, p):
            if not valid(t, NT):
                return
            wait(dve, x_sc, t + 1)
            dve.reduce_max(mx[:, p, :], ps[:, p, 0:S], AX.X).then_inc(x_max, 1)
            dve.wait_ge(x_max, t + 1)
            dve.tensor_scalar(nmx[:, p, :], mx[:, p, :], -(D ** -0.5), None, ALU.mult).then_inc(x_nmax, 1)

        def last_row(t, p):
            if not valid(t, NT):
                return
            wait(dve, x_exp, t + 1)
            dve.reciprocal(rrs[:, p, :], rs[:, p, :])
            dve.tensor_scalar(p_last[:, p, :], con[:, C_BATCH:C_BATCH + BT], prob[:, p, S - 1:S], None,
                              ALU.mult).then_inc(x_plast, 1)

        def norm(t, p):
            if not valid(t, NT):
                return
            wait(dve, x_pv, t + 1)
            wait(dve, x_plast, t + 1)
            wait(dve, x_ct, t)
            dve.tensor_scalar(cn[:, :], ps[:, 5, 0:D], rrs[:, p, :], None, ALU.mult).then_inc(x_norm, 1)

        def x1(t, p):
            if not valid(t, NT):
                return
            wait(dve, x_out, t + 1)
            wait(dve, x_bias, t + 1)
            dve.tensor_tensor(row(t), ps[:, 7, 0:D], row(t), ALU.add).then_inc(x_x1, 1)

        def xstep(t, p):
            maxes(t, p)
            last_row(t, p)
            norm(t - 1, 1 - p)
            x1(t - 2, p)
            if valid(t - 2, NT):
                wait(dve, x_x1, t - 1)
            ln(t + 3, 1 - p)
            if valid(t - 2, NT):
                stats_of(t - 2, 1, x_bn)

        skewed(dve, xstep, -3, X_LO, X_HI, NT + 2)

        variance(1, x_bn)

        def a_lns(r):
            wait(dve, a_tr, r)
            for s in range(2):
                normed(xn2[:, s, :], 2 * r + s, 1, a_ln)

        def a_lo_ev(r):
            wait(dve, a_hi, r + 1)
            dve.tensor_tensor(xT_lo[:, :, :], ps[:, 4, :].rearrange("p (c d) -> p c d", c=DC), xT_hi[:, :, :].bitcast(F32),
                              ALU.subtract).then_inc(a_lo, 1)

        def elus(r):
            for n in range(8):
                if n == 7:
                    wait(dve, a_x2, 2 * r)
                wait(dve, a_e, 8 * r + n + 1)
                dve.tensor_scalar(ex[:, n % 2, :], ex[:, n % 2, :], 1.0, None, ALU.min).then_inc(a_emin, 1)
                dve.wait_ge(a_emin, 8 * r + n + 1)
                if n < 4:
                    for hh in range(2):
                        lo, hi = hh * HD, (hh + 1) * HD
                        m = dve.scalar_tensor_tensor(
                            q_pad[lo:hi, 2 * n:2 * n + 2, hh, :, :].rearrange("p c s t -> p c (s t)"),
                            ps[lo:hi, n % 4, :].rearrange("p (c n) -> p c n", c=2), 0.0,
                            ex[lo:hi, n % 2, :].rearrange("p (c n) -> p c n", c=2), ALU.max, ALU.add)
                else:
                    c = 2 * (n - 4)
                    m = dve.scalar_tensor_tensor(kT[:, c:c + 2, :].rearrange("p c n -> p (c n)"), ps[:, n % 4, :], 0.0,
                                                 ex[:, n % 2, :], ALU.max, ALU.add)
                m.then_inc(a_qku, 1)

        def masks(r):
            mask = con[:, C_MASK:C_MASK + P].rearrange("p (a t) -> p a t", a=1).to_broadcast([P, 4, P])
            for n in range(8):
                s, m4 = n // 4, n % 4
                wait(dve, a_sc, 8 * r + n + 1)
                dve.tensor_tensor(att[:, s, 4 * m4:4 * m4 + 4, :], ps[:, n % 4, :].rearrange("p (h t) -> p h t", h=4),
                                  mask, ALU.mult).then_inc(a_scu, 1)

        def gates(r, s):
            for n in range(4 * s, 4 * s + 4):
                b = n % 2
                wait(dve, a_avu, 8 * r + n - 1)
                wait(dve, a_av, 8 * r + n + 1)
                num = ps[:, n % 4, :].rearrange("p (h t) -> p h t", h=4)
                g4 = slice((n % 4) * 4 * HD, (n % 4 + 1) * 4 * HD)
                dve.tensor_scalar(dn[:, b, :, :], num[:, :, HD:V1], DEN_EPS, None, ALU.add).then_inc(a_dn, 1)
                dve.tensor_tensor(gn[:, b, :, :], eg[:, s, g4].rearrange("p (h t) -> p h t", h=4), num[:, :, 0:HD],
                                  ALU.mult).then_inc(a_gn, 1)
                dve.wait_ge(a_dn, 8 * r + n + 1)
                dve.reciprocal(rdn[:, b, :, :], dn[:, b, :, :]).then_inc(a_rdn, 1)
                dve.wait_ge(a_gn, 8 * r + n + 1)
                dve.wait_ge(a_rdn, 8 * r + n + 1)
                dve.tensor_tensor(o_sb[:, s, g4].rearrange("p (h t) -> p h t", h=4), gn[:, b, :, :],
                                  rdn[:, b, :, :].to_broadcast([P, 4, HD]), ALU.mult).then_inc(a_avu, 1)

        def x2(r, s):
            t = 2 * r + s
            wait(dve, a_y, t + 1)
            dve.tensor_tensor(row(t), ps[:, 7, 0:D], row(t), ALU.add).then_inc(a_x2, 1)

        def astep(r, more=True):
            elus(r)
            if valid(r - 1, NT):
                for s in range(2):
                    stats_of(2 * (r - 1) + s, 2, a_bn)
            if more:
                a_lns(r + 1)
            masks(r)
            gates(r, 0)
            gates(r, 1)
            if more:
                a_lo_ev(r + 1)
            x2(r, 0)
            x2(r, 1)

        a_lns(0)
        dve.wait_ge(s_split_lo, NPIECE)
        dve.wait_ge(l_z, 32)
        dve.memset(q_pad[:, :, :, :, :].rearrange("p c h s t -> p (c h s t)"), 0.0).then_inc(a_init, 1)
        dve.memset(v_one[:, :, :].rearrange("p s w -> p (s w)"), 1.0).then_inc(a_init, 1)
        dve.wait_ge(a_init, 2)
        a_lo_ev(0)
        astep(0)
        with dve.Fori(1, NT // 2 - 1) as r:
            astep(r)
        astep(NT // 2 - 1, False)

        def up_lo(t, cs, e):
            if not valid(t, SLOT_TILES):
                return
            for c in cs:
                wait(dve, f_uhi, 4 * t + c + 1)
                dve.tensor_tensor(w_lo[:, c, :].rearrange("p (c n) -> p c n", c=DC),
                                  w13[:, bass.ds(e, 1), c % 2, :, c // 2 * 512:(c // 2 + 1) * 512].rearrange("p a c n -> p (a c) n"),
                                  w_hi[:, c, :].bitcast(F32).rearrange("p (c n) -> p c n", c=DC), ALU.subtract).then_inc(f_ulo, 1)

        def expert(t):
            return dve.value_load(tile_e[0:1, bass.ds(t, 1)], min_val=0, max_val=E - 1) if valid(t, SLOT_TILES) else None

        dve.wait_ge(a_x2, NT)
        for s in range(2):
            stats_of(NT - 2 + s, 2, a_bn)
        variance(2, a_bn)

        def g_lns(t, p):
            if not valid(t, NT):
                return
            normed(xn3[:, bass.ds(t, 1), :].rearrange("p a d -> p (a d)"), t, 2, g_ln)

        def pick(t, p):
            if not valid(t, NT):
                return
            wait(dve, g_mm, t + 1)
            dve.tensor_copy(sc[:, bass.ds(t, 1), :].rearrange("p a n -> p (a n)"), ps[:, 2 + p, 0:E]).then_inc(g_sc, 1)

        def gstep(t, p):
            g_lns(t + 2, p)
            pick(t, p)

        skewed(dve, gstep, -2, 4, NT - 2, NT)
        dve.wait_ge(g_sc, NT)
        for t in range(NT):
            dve.max(m8[:, t, :], sc[:, t, :]).then_inc(g_max, 1)
        dve.wait_ge(g_max, NT)
        for t in range(NT):
            dve.max_index(i8[:, t, :], m8[:, t, :], sc[:, t, :]).then_inc(g_idx, 1)
        dve.wait_ge(g_idx, NT)

        steps = [0]

        def link(m):
            steps[0] += 1
            m.then_inc(r_step, 1)
            dve.wait_ge(r_step, steps[0])

        dve.tensor_tensor(dv[:, :], m8[:, :, 1], m8[:, :, 0], ALU.subtract).then_inc(r_d, 1)
        link(dve.tensor_copy(i8f[:, :, :], i8[:, :, :]))
        iota = con[:, C_IOTA:C_IOTA + E].rearrange("p (a e) -> p a e", a=1).to_broadcast([P, NT, E])
        for k, dst in enumerate((first, second)):
            link(dve.tensor_tensor(dst[:, :, :], i8f[:, :, k:k + 1].to_broadcast([P, NT, E]), iota, ALU.is_equal))
        dve.tensor_tensor(both[:, :, :], first[:, :, :], second[:, :, :], ALU.add).then_inc(r_sum, 1)
        for b in scan:
            link(dve.memset(b[:, 0:8, :], 0.0))
        for b in tiles:
            link(dve.memset(b[:, 0:4], 0.0))
        dve.wait_ge(r_e1, 1)
        link(dve.tensor_scalar(dv[:, :], e1[:, :], 1.0, None, ALU.add))
        link(dve.reciprocal(top_w[:, 0, :], dv[:, :]))
        link(dve.tensor_tensor(top_w[:, 1, :], e1[:, :], top_w[:, 0, :], ALU.mult))
        dve.wait_ge(r_sum, 2)
        link(dve.tensor_copy(scan[0][:, 8:, :], ps[:, 5, 0:NT * E].rearrange("p (t e) -> p t e", e=E)))
        cur = 0
        for d in (1, 2, 4, 8):
            link(dve.tensor_tensor(scan[1 - cur][:, 8:, :], scan[cur][:, 8:, :], scan[cur][:, 8 - d:8 - d + NT, :], ALU.add))
            cur = 1 - cur
        seen = scan[cur]
        total = seen[:, 8 + NT - 1, :]
        link(dve.tensor_tensor(cmp[:, :, :], total.rearrange("p (e a) -> p e a", a=1).to_broadcast([P, E, MAXT]),
                               con[:, C_STEP:C_STEP + MAXT].rearrange("p (a m) -> p a m", a=1).to_broadcast([P, E, MAXT]),
                               ALU.is_gt))
        link(dve.reduce_sum(tiles[0][:, 4:], cmp[:, :, :], AX.X))
        cur = 0
        for d in (1, 2, 4):
            link(dve.tensor_tensor(tiles[1 - cur][:, 4:], tiles[cur][:, 4:], tiles[cur][:, 4 - d:4 - d + E], ALU.add))
            cur = 1 - cur
        end = tiles[cur]
        link(dve.tensor_tensor(cmp2[:, :, :], con[:, C_TILE:C_TILE + SLOT_TILES].rearrange("p (t a) -> p t a", a=1).to_broadcast([P, SLOT_TILES, E]),
                               end[:, 4:].rearrange("p (a e) -> p a e", a=1).to_broadcast([P, SLOT_TILES, E]), ALU.is_ge))
        link(dve.reduce_sum(tef[:, :], cmp2[:, :, :], AX.X))
        dve.tensor_scalar(tile_e[:, :], tef[:, :], float(E - 1), None, ALU.min).then_inc(r_map, 1)
        dve.wait_ge(r_map, 1)
        link(dve.tensor_tensor(slot[:, :, :], ps[:, 4, 0:NT * E].rearrange("p (t e) -> p t e", e=E), seen[:, 7:7 + NT, :], ALU.add))
        link(dve.scalar_tensor_tensor(slot[:, :, :], end[:, 3:3 + E].rearrange("p (a e) -> p a e", a=1).to_broadcast([P, NT, E]),
                                      float(P), slot[:, :, :], ALU.mult, ALU.add))
        for k, chosen in enumerate((first, second)):
            link(dve.tensor_tensor(prod[:, :, :], chosen[:, :, :], slot[:, :, :], ALU.mult))
            link(dve.reduce_sum(posf[:, k * NT:(k + 1) * NT], prod[:, :, :], AX.X))
        link(dve.tensor_copy(pos[:, :], posf[:, :]))
        dve.tensor_scalar(pos_tile[:, :], pos[:, :], P.bit_length() - 1, None, ALU.logical_shift_right).then_inc(r_step, 1)
        dve.tensor_scalar(pos_in[:, :], pos[:, :], P - 1, None, ALU.bitwise_and).then_inc(r_step, 1)
        steps[0] += 2
        dve.wait_ge(r_step, steps[0])
        dve.tensor_copy(tilef[:, :], pos_tile[:, :]).then_inc(r_step, 1)
        dve.tensor_copy(inf[:, :], pos_in[:, :]).then_inc(r_step, 1)
        steps[0] += 2
        dve.wait_ge(r_step, steps[0])
        link(dve.tensor_tensor(in_tile[:, :, :], con[:, C_TILE:C_TILE + SLOT_TILES].rearrange("p (a t) -> p a t", a=1).to_broadcast([P, TOP * NT, SLOT_TILES]),
                               tilef[:, :].rearrange("p (n a) -> p n a", a=1).to_broadcast([P, TOP * NT, SLOT_TILES]), ALU.is_equal))
        for k in range(TOP):
            half_ = slice(k * NT, (k + 1) * NT)
            dve.tensor_tensor(what[:, half_, 0, :], in_tile[:, half_, :],
                              con[:, C_ID1:C_ID1 + NT].rearrange("p (t a) -> p t a", a=1).to_broadcast([P, NT, SLOT_TILES]),
                              ALU.mult)
            dve.tensor_tensor(what[:, half_, 1, :], in_tile[:, half_, :],
                              top_w[:, k, :].rearrange("p (t a) -> p t a", a=1).to_broadcast([P, NT, SLOT_TILES]), ALU.mult)
        for q in range(TOP * NT // 4):
            wait(dve, r_tab, q - IN_SLOTS + 1)
            dve.tensor_tensor(in_slot[:, q % IN_SLOTS, :, :], con[:, C_I128:C_I128 + P].rearrange("p (a s) -> p a s", a=1).to_broadcast([P, 4, P]),
                              inf[:, 4 * q:4 * q + 4].rearrange("p (n a) -> p n a", a=1).to_broadcast([P, 4, P]),
                              ALU.is_equal).then_inc(r_in, 1)
        up_lo(0, range(4), expert(0))
        dve.wait_ge(r_tab, TOP * NT // 4)
        link(dve.tensor_scalar(spare[:, :], ps[:, 6, 0:SLOT_TILES], 0.0, con[:, C_SPARE1:C_SPARE1 + 1], ALU.is_equal, ALU.mult))
        link(dve.tensor_copy(slot_w[:, :], ps[:, 6, SLOT_TILES:2 * SLOT_TILES]))
        dve.scalar_tensor_tensor(slot_row[:, :], ps[:, 6, 0:SLOT_TILES], -1.0, spare[:, :], ALU.add, ALU.add).then_inc(r_done, 1)

        def down_hi(t):
            if not valid(t, SLOT_TILES):
                return
            wait(dve, f_w2[1], 16 * (t + 1))
            wait(dve, f_dn, 2 * t)
            dve.tensor_copy(w_hi[:, 5, :], w2_sb[:, HC // 2:, :].rearrange("p c d -> p (c d)")).then_inc(f_dhi1, 1)

        def times(t, j):
            if not valid(t, SLOT_TILES):
                return
            wait(dve, f_up, 4 * t + 2 * j + 2)
            wait(dve, f_silu, 2 * t + j + 1)
            cols = slice(j * 512, (j + 1) * 512)
            dve.tensor_tensor(h_sb[:, cols], h_sb[:, cols], ps[:, 2 * j + 1, :], ALU.mult).then_inc(f_h, 1)

        def x_lo(t):
            if not valid(t, SLOT_TILES):
                return
            wait(dve, f_xh, t + 1)
            dve.tensor_tensor(xl[:, :, :], ps[:, 6, 0:D].rearrange("p (c d) -> p c d", c=DC), xh[:, :, :].bitcast(F32),
                              ALU.subtract).then_inc(f_xl, 1)

        def h_lo(t):
            if not valid(t, SLOT_TILES):
                return
            wait(dve, f_hh, t + 1)
            dve.tensor_tensor(hl[:, :, :], ps[:, 4:6, :].rearrange("p a (c d) -> p (a c) d", c=4), hh[:, :, :].bitcast(F32),
                              ALU.subtract).then_inc(f_hl, 1)

        def fstep(t):
            e = expert(t + 1)
            times(t, 0)
            up_lo(t + 1, (0, 1), e)
            times(t, 1)
            up_lo(t + 1, (2,), e)
            x_lo(t + 1)
            up_lo(t + 1, (3,), e)
            down_hi(t)
            h_lo(t)

        x_lo(0)
        for t in range(2):
            fstep(t)
        with dve.Fori(2, SLOT_TILES - 1) as t:
            fstep(t)
        for t in range(SLOT_TILES - 1, SLOT_TILES + 1):
            fstep(t)


def kernel(x, ctx_1024, L0_xattn_Wk, L0_xattn_Wv, L0_xattn_bv, L0_xattn_Wq, L0_xattn_bq, L0_xattn_Wo, L0_xattn_bo,
           L0_attn_w_qkv, L0_attn_w_gate, L0_attn_w_out, L0_ffn_gate_w, L0_ffn_w1, L0_ffn_w2, L0_ffn_w3):
    import concourse.bacc as bacc
    from concourse.bass_utils import run_bass_kernel_spmd

    ctx4 = np.asarray(ctx_1024).reshape(NT, BT, S, D)
    w1, w3, w2 = (np.asarray(w) for w in (L0_ffn_w1, L0_ffn_w3, L0_ffn_w2))
    arrays = {
        "con": constants(),
        "x": np.asarray(x).reshape(NT, P, D).transpose(1, 0, 2),
        "ctxT": ctx4.transpose(0, 3, 1, 2).reshape(NT, DC, P, BT, S).transpose(0, 2, 3, 1, 4).reshape(NT, P, BT * DC * S),
        "ctxN": ctx4[:, :, :KC * P].reshape(NT, BT, KC, P, D).transpose(0, 3, 1, 2, 4).reshape(NT, P, BT * KC * D),
        "ctxL": ctx4[:, :, S - 1],
        "Wq": np.asarray(L0_xattn_Wq), "Wk": np.asarray(L0_xattn_Wk), "Wv": np.asarray(L0_xattn_Wv),
        "WoT": np.asarray(L0_xattn_Wo).T,
        "bq": np.asarray(L0_xattn_bq).reshape(DC, P).T, "bv": np.asarray(L0_xattn_bv).reshape(DC, P).T,
        "bo": np.asarray(L0_xattn_bo).reshape(1, D),
        "w_a": np.concatenate([np.asarray(L0_attn_w_qkv), np.asarray(L0_attn_w_gate)], axis=1)
                 .reshape(DC, P, 4 * HF).transpose(1, 0, 2).reshape(P, DC * 4 * HF),
        "w_out": np.asarray(L0_attn_w_out),
        "gate": np.asarray(L0_ffn_gate_w).T,
        "w13": np.stack([w1, w3], axis=1).reshape(E, 2, HID, DC, P).transpose(0, 4, 1, 3, 2).reshape(E, P, 2 * DC * HID),
        "w2": w2.reshape(E, D, HC, P).transpose(0, 3, 2, 1).reshape(E, P, HC * D),
    }
    nc = bacc.Bacc("TRN2", target_bir_lowering=False, num_devices=1)
    ins, args = {}, {}
    for name, value in arrays.items():
        value = np.ascontiguousarray(value)
        ins[f"in_{name}"] = value
        args[name] = nc.dram_tensor(f"in_{name}", value.shape, F32, kind="ExternalInput").ap()
    out = nc.dram_tensor("out_x", ((NT + 1) * P, D), F32, kind="ExternalOutput").ap()
    program(nc, args, out)
    r = run_bass_kernel_spmd(nc, [ins], core_ids=[0])
    return r.results[0]["out_x"][:B * T].reshape(B, T, D)
```
